# Optimizing a Trainium2 kernel written in Bass

```python
import numpy as np
import jax
import jax.numpy as jnp

def _softmax(x, axis=-1):
    return jax.nn.softmax(x, axis=axis)

def _gelu(x):
    return jax.nn.gelu(x, approximate=True)

def _silu(x):
    return jax.nn.silu(x)

def _sigmoid(x):
    return jax.nn.sigmoid(x)

def _layernorm(x, axis=-1, eps=1e-05):
    m = jnp.mean(x, axis=axis, keepdims=True)
    v = jnp.var(x, axis=axis, keepdims=True)
    return (x - m) / jnp.sqrt(v + eps)

def _scatter_add(tgt, idx, src, axis=0):
    return tgt.at[idx].add(src)

def _segment_sum(src, seg, n):
    return jax.ops.segment_sum(src, seg, n)
kernel_name = 'mk_seq_preln_d1_jaxref_r8_2a67a3'

def setup_inputs(seed: int=0):
    np.random.seed(seed)
    _w = jnp.asarray

    def _L0_attn_setup():
        import jax, jax.numpy as jnp
        import numpy as np
        EMBED_DIM = 128
        NUM_HEADS = 16
        HEAD_DIM = EMBED_DIM // NUM_HEADS
        NUM_DECAYS = 2
        BATCH = 2
        SEQ = 256
        W_SCALE = 0.02
        key = jax.random.key(seed)
        ks = jax.random.split(key, 12)
        d = EMBED_DIM
        inp = {'x': jax.random.normal(ks[0], (BATCH, SEQ, d), dtype=jnp.float32), 'Wq': jax.random.normal(ks[1], (d, d), dtype=jnp.float32) * W_SCALE, 'bq': jnp.zeros((d,), dtype=jnp.float32), 'Wk': jax.random.normal(ks[2], (d, d), dtype=jnp.float32) * W_SCALE, 'bk': jnp.zeros((d,), dtype=jnp.float32), 'Wv': jax.random.normal(ks[3], (d, d), dtype=jnp.float32) * W_SCALE, 'bv': jnp.zeros((d,), dtype=jnp.float32), 'Wo': jax.random.normal(ks[4], (d, d), dtype=jnp.float32) * W_SCALE, 'bo': jnp.zeros((d,), dtype=jnp.float32), 'decay_params': jax.random.uniform(ks[5], (NUM_HEADS, NUM_DECAYS), dtype=jnp.float32), 'mix_weights': jax.random.normal(ks[6], (NUM_HEADS, NUM_DECAYS), dtype=jnp.float32)}
        return inp
    _L0_attn_in = _L0_attn_setup()

    def _L0_ffn_setup():
        import jax, jax.numpy as jnp
        import numpy as np
        TOP_P = 0.8
        B, T, H, F, E = (2, 256, 128, 512, 8)
        key = jax.random.key(seed)
        k0, k1, k2, k3 = jax.random.split(key, 4)
        x = jax.random.normal(k0, (B, T, H), jnp.float32)
        Wr = jax.random.normal(k1, (H, E), jnp.float32) * 0.02
        br = jnp.zeros((E,), jnp.float32)
        W1 = jax.random.normal(k2, (E, H, F), jnp.float32) * 0.02
        b1 = jnp.zeros((E, F), jnp.float32)
        W2 = jax.random.normal(k3, (E, F, H), jnp.float32) * 0.02
        b2 = jnp.zeros((E, H), jnp.float32)
        return {'x': x, 'Wr': Wr, 'br': br, 'W1': W1, 'b1': b1, 'W2': W2, 'b2': b2}
    _L0_ffn_in = _L0_ffn_setup()
    _d = {'L0_attn_x': _L0_attn_in['x'], 'L0_attn_Wq': _L0_attn_in['Wq'], 'L0_attn_bq': _L0_attn_in['bq'], 'L0_attn_Wk': _L0_attn_in['Wk'], 'L0_attn_bk': _L0_attn_in['bk'], 'L0_attn_Wv': _L0_attn_in['Wv'], 'L0_attn_bv': _L0_attn_in['bv'], 'L0_attn_Wo': _L0_attn_in['Wo'], 'L0_attn_bo': _L0_attn_in['bo'], 'L0_attn_decay_params': _L0_attn_in['decay_params'], 'L0_attn_mix_weights': _L0_attn_in['mix_weights'], 'L0_ffn_Wr': _L0_ffn_in['Wr'], 'L0_ffn_br': _L0_ffn_in['br'], 'L0_ffn_W1': _L0_ffn_in['W1'], 'L0_ffn_b1': _L0_ffn_in['b1'], 'L0_ffn_W2': _L0_ffn_in['W2'], 'L0_ffn_b2': _L0_ffn_in['b2']}
    _x0 = _d['L0_attn_x']
    _d['L0_attn_x'] = jax.random.normal(jax.random.fold_in(jax.random.key(seed), 1), (1, 2048, 128), dtype=_x0.dtype)
    del _x0
    return _d

def reference(L0_attn_x, L0_attn_Wq, L0_attn_bq, L0_attn_Wk, L0_attn_bk, L0_attn_Wv, L0_attn_bv, L0_attn_Wo, L0_attn_bo, L0_attn_decay_params, L0_attn_mix_weights, L0_ffn_Wr, L0_ffn_br, L0_ffn_W1, L0_ffn_b1, L0_ffn_W2, L0_ffn_b2):

    def _L0_attn_ref(x, Wq, bq, Wk, bk, Wv, bv, Wo, bo, decay_params, mix_weights):
        import jax, jax.numpy as jnp
        import numpy as np
        EMBED_DIM = 128
        NUM_HEADS = 16
        HEAD_DIM = EMBED_DIM // NUM_HEADS
        NUM_DECAYS = 2
        BATCH = 2
        SEQ = 256
        W_SCALE = 0.02
        B, S, _ = x.shape
        H, D = (NUM_HEADS, HEAD_DIM)

        def proj(W, b):
            return (jnp.einsum('bse,fe->bsf', x, W) + b).reshape(B, S, H, D).transpose(0, 2, 1, 3)
        q = proj(Wq, bq)
        k = proj(Wk, bk)
        v = proj(Wv, bv)
        attn_scores = jnp.einsum('bhqd,bhkd->bhqk', q, k) / jnp.sqrt(jnp.float32(D))
        t = jnp.arange(S, dtype=jnp.float32)
        time_diffs = jnp.abs(t[:, None] - t[None, :])
        dp = jnp.clip(decay_params, 0.01, 0.9999)
        decay_masks = dp[:, :, None, None] ** time_diffs[None, None, :, :]
        mix = jax.nn.softmax(mix_weights, axis=-1)
        decay_mask = jnp.einsum('hnqk,hn->hqk', decay_masks, mix)
        attn_scores = attn_scores * decay_mask[None]
        attn_probs = jax.nn.softmax(attn_scores, axis=-1)
        out = jnp.einsum('bhqk,bhkd->bhqd', attn_probs, v)
        out = out.transpose(0, 2, 1, 3).reshape(B, S, H * D)
        return jnp.einsum('bse,fe->bsf', out, Wo) + bo

    def _L0_ffn_ref(x, Wr, br, W1, b1, W2, b2):
        import jax, jax.numpy as jnp
        import numpy as np
        TOP_P = 0.8
        B, T, H, F, E = (2, 256, 128, 512, 8)
        probs = jax.nn.softmax(x @ Wr + br, axis=-1)
        sorted_idx = jnp.argsort(-probs, axis=-1)
        sorted_probs = jnp.take_along_axis(probs, sorted_idx, axis=-1)
        cum = jnp.cumsum(sorted_probs, axis=-1)
        mask = cum < TOP_P
        mask = mask.at[..., 0].set(True)
        inv = jnp.argsort(sorted_idx, axis=-1)
        keep = jnp.take_along_axis(mask, inv, axis=-1)
        gate = probs * keep
        h = jax.nn.relu(jnp.einsum('bth,ehf->betf', x, W1) + b1[None, :, None, :])
        y = jnp.einsum('betf,efh->beth', h, W2) + b2[None, :, None, :]
        return jnp.einsum('bte,beth->bth', gate, y)
    x = L0_attn_x
    x = x + _L0_attn_ref(_layernorm(x, axis=-1), L0_attn_Wq, L0_attn_bq, L0_attn_Wk, L0_attn_bk, L0_attn_Wv, L0_attn_bv, L0_attn_Wo, L0_attn_bo, L0_attn_decay_params, L0_attn_mix_weights)
    x = x + _L0_ffn_ref(_layernorm(x, axis=-1), L0_ffn_Wr, L0_ffn_br, L0_ffn_W1, L0_ffn_b1, L0_ffn_W2, L0_ffn_b2)
    return x

_drawn_inputs = setup_inputs


def setup_inputs(seed=0):
    import zlib

    import numpy as np

    out = dict(_drawn_inputs(seed))
    spreads = {'L0_attn_bq': (0.0, 0.8),
     'L0_attn_bk': (0.0, 0.8),
     'L0_attn_bv': (0.0, 0.378),
     'L0_attn_bo': (0.0, 0.1),
     'L0_ffn_br': (0.0, 0.389),
     'L0_ffn_b1': (0.0, 0.8),
     'L0_ffn_b2': (0.0, 0.268)}
    factors = {'L0_attn_Wq': 8.0,
     'L0_attn_Wk': 8.0,
     'L0_attn_Wv': 8.0,
     'L0_attn_decay_params': 8.0,
     'L0_attn_mix_weights': 8.0,
     'L0_ffn_W1': 2.807}
    for name, (base, spread) in spreads.items():
        noise = np.random.default_rng([zlib.crc32(name.encode()), seed]).standard_normal(out[name].shape)
        drawn = base * np.exp(spread * noise) if base else spread * noise
        out[name] = jnp.asarray(drawn.astype(out[name].dtype))
    for name, factor in factors.items():
        out[name] = (out[name] * factor).astype(out[name].dtype)
    return out
```

```python
from contextlib import ExitStack

import numpy as np

import concourse.bass as bass
from concourse import mybir

ALU = mybir.AluOpType
ACT = mybir.ActivationFunctionType
AX = mybir.AxisListType
F32 = mybir.dt.float32
BF16 = mybir.dt.bfloat16
F16 = mybir.dt.float16

P = 128
S = 2048
E = 128
H, D, N = 16, 8, 2
T = S // P
QB = 512
NB = S // QB
BT = QB // P
X, F = 8, 512
FC = F // P
EPS = 1e-5
TOP_P = 0.8

WIDTHS = (1024, 512, 256, 128)
LV = len(WIDTHS)
V = LV + 1
ROWS = N * D
PAIRS = ((0, 0), (0, 1), (1, 0), (1, 1), (0, 2), (2, 0))
KR = len(PAIRS) * ROWS
SH = KR + 3

ASLOTS, BSLOTS, PSLOTS = 3, 3, 4
U = 3
STEPS_IN_LOOP = 12
LAG = 3
AHEAD = 8
UNITS = T * NB


def block_pieces(own, other, tile):
    if own != other:
        v = 0 if own // 2 != other // 2 else 1
        return [(v, 0, QB)]
    a = tile % BT
    return [(2, 256 * (1 - a // 2), 256), (3, 128 * (a ^ 1), 128), (V - 1, 128 * a, 128)]


def key_order(block):
    diag = [BT * block + a for a in range(BT)]
    rest = [j for j in range(T) if j // BT != block]
    out = []
    for a in range(BT):
        out += rest[3 * a:3 * a + 2] + [diag[a]] + rest[3 * a + 2:3 * a + 3]
    return out


def build_program(nc, a, out):
    ctx = ExitStack()
    with ctx:
        def sb(name, shape, dt=F32):
            return ctx.enter_context(nc.sbuf_tensor(name, shape, dt))

        def sem(name):
            return ctx.enter_context(nc.semaphore(name))

        xn = sb("xn", [P, T, E])
        xT = sb("xT", [P, S])
        ident = sb("ident", [P, P])
        identb = sb("identb", [P, P], BF16)
        dist = sb("dist", [P, LV * QB], F16)
        absd = sb("absd", [P, P])
        cols = sb("cols", [P, 8])
        wqk = sb("wqk", [P, H, 2 * ROWS])
        wv = sb("wv", [P, E])
        wo = sb("wo", [P, E])
        bvo = sb("bvo", [P, 2, E])
        bqk = sb("bqk", [P, H])
        dec = sb("dec", [P, H + 2 * H])
        mixw = sb("mixw", [P, H, N])
        mixs = sb("mixs", [P, 3, H])
        mixt = sb("mixt", [P, H, 1 + N])
        mixh = sb("mixh", [P, 1 + N])
        stats = sb("stats", [P, T, 6])
        mv = sb("mv", [P, T, 2])
        rstd = sb("rstd", [P, T])
        wst = sb("wst", [P, 2 * ROWS])
        base = sb("base", [P, QB])
        basem = sb("basem", [P, QB])
        xs = sb("xs", [P, V, QB])
        parts = sb("parts", [P, 3, V, QB], BF16)
        stage = [sb(f"stage{s}", [P, 2, V, S], BF16) for s in range(U)]
        masks = sb("masks", [P, U, P])
        maske = sb("maske", [P, 2, P])
        vals = sb("vals", [P, T, H, D])
        vh = sb("vh", [P, U, T, 32])
        probs = sb("probs", [P, PSLOTS, QB])
        pvs = sb("pvs", [P, 2, QB])
        mx = sb("mx", [P, T * NB])
        nm = sb("nm", [P, 2, T])
        nmp = sb("nmp", [P, 3, T], BF16)
        nmT = sb("nmT", [3 * T, P], BF16)
        ou = sb("ou", [P, T, D + 1])
        rz = sb("rz", [P, T])

        SA = [ctx.enter_context(nc.psum_tensor(f"SA{i}", [P, QB], F32)) for i in range(ASLOTS)]
        SB = [ctx.enter_context(nc.psum_tensor(f"SB{i}", [P, QB], F32)) for i in range(BSLOTS)]
        PV = ctx.enter_context(nc.psum_tensor("PV", [P, QB], F32))
        MISC = ctx.enter_context(nc.psum_tensor("MISC", [P, QB], F32))

        in_x = [sem(f"in_x{i}") for i in range(NB)]
        in_c = sem("in_c")
        passed = sem("passed")
        ones_set = sem("ones_set")
        bn_done = sem("bn_done")
        rstd_ready = sem("rstd_ready")
        sqrt_done = sem("sqrt_done")
        normed = sem("normed")
        transposed = sem("transposed")
        xT_ready = sem("xT_ready")
        v_made = sem("v_made")
        v_ready = sem("v_ready")
        small = sem("small")
        small_act = sem("small_act")
        tables = sem("tables")

        wst_ready = sem("wst_ready")
        base_made = sem("base_made")
        base_ready = sem("base_ready")
        fac_ready = sem("fac_ready")
        maske_ready = sem("maske_ready")
        xs_ready = sem("xs_ready")
        high_ready = sem("high_ready")
        pool_chain = sem("pool_chain")
        parts_ready = sem("parts_ready")
        mask_ready = sem("mask_ready")
        staged = [sem(f"staged{s}") for s in range(U)]
        shifted = [sem(f"shifted{s}") for s in range(U)]

        a_made = sem("a_made")
        a_free = sem("a_free")
        a_masked = sem("a_masked")
        b_plain = sem("b_plain")
        b_raw = sem("b_raw")
        b_masked = sem("b_masked")
        b_diag = sem("b_diag")
        exp_done = sem("exp_done")
        pv_used = sem("pv_used")
        pv_out = sem("pv_out")
        pvs_free = sem("pvs_free")
        ou_step = sem("ou_step")
        rz_ready = sem("rz_ready")
        o_ready = sem("o_ready")
        nm_step = sem("nm_step")
        nmT_made = sem("nmT_made")
        nmT_ready = sem("nmT_ready")

        x1_in, w1_in, w2_in = sem("x1_in"), sem("w1_in"), sem("w2_in")
        oT_made, oT_ready = sem("oT_made"), sem("oT_ready")
        wo_made, x1_ready = sem("wo_made"), sem("x1_ready")
        lg_ready = sem("lg_ready")
        rt_made, rt_step, rt_act = sem("rt_made"), sem("rt_step"), sem("rt_act")
        gT_made, gT_ready = sem("gT_made"), sem("gT_ready")
        g_out, g_in = sem("g_out"), sem("g_in")
        up_made, up_scaled, h_ready = sem("up_made"), sem("up_scaled"), sem("h_ready")
        h_free = sem("h_free")
        y_out, yT_made, y_done, stored = sem("y_out"), sem("yT_made"), sem("y_done"), sem("stored")

        n_consts = 14 * 16

        class Turn:
            def __init__(self, eng, index, value):
                self.eng, self.index, self.value = eng, index, value

        def count(it, per_head, n):
            if it is None:
                return n
            it.eng.reg_add(it.value, it.index * (U * per_head), n)
            return it.value

        def apart(eng):
            eng.sem_inc(passed, 1)

        def head(it, k):
            return k if it is None else it.index * U + k

        def gathered(it, k):
            return count(it, 16 * 2 * len(PAIRS) * NB // U, (k // U + 1) * (16 * 2 * len(PAIRS) * NB))

        def shifts(it, k):
            return count(it, 16 * 3 * V // U, (k // U + 1) * (16 * 3 * V))

        def steps(eng, body):
            value = eng.alloc_register("wait_value")
            with eng.Fori(0, STEPS_IN_LOOP // U) as index:
                for k in range(U):
                    body(Turn(eng, index, value), k)
            for h in range(STEPS_IN_LOOP, H):
                body(None, h)

        def timeline(it, k):
            last_a = H * UNITS
            seq = []
            for n in range(UNITS):
                seq.append(("b", n))
                if n >= 1:
                    seq.append(("shift", n - 1))
                seq.append(("a", n))
                if n == UNITS - AHEAD:
                    seq.append(("finish", 0))
                if n == UNITS - AHEAD + 3:
                    seq.append(("maxima", 0))
                if n >= LAG:
                    seq.append(("pv", n - LAG))
                if n == 4:
                    seq.append(("base", 0))
                m = n - LAG - 5
                if m > 0 and m % T == T - 1:
                    seq.append(("sum", m // T))
            seq.append(("shift", UNITS - 1))
            for n in range(UNITS - LAG, UNITS):
                seq.append(("pv", n))
            seq.append(("sum", NB - 1))
            h = None if it is not None else k
            if h is not None:
                keep = []
                for what, n in seq:
                    if what == "a" and UNITS * (h + 1) + AHEAD + n >= last_a:
                        continue
                    if what in ("finish", "maxima") and h + 1 >= H:
                        continue
                    if what == "base" and h + U >= H:
                        continue
                    keep.append((what, n))
                seq = keep
            return seq

        def widen(ap, n):
            return ap.unsqueeze(2).broadcast_to([P, T, n])

        f0 = stage[0][:, :, :, :].rearrange("p a v s -> p (a v s)").bitcast(F32)
        f1 = stage[1][:, :, :, :].rearrange("p a v s -> p (a v s)").bitcast(F32)
        f2 = stage[2][:, :, :, :].rearrange("p a v s -> p (a v s)").bitcast(F32)
        FW = X * F
        x = f2[:, 0:T * E].rearrange("p (t e) -> p t e", e=E)
        x1 = vals[:].rearrange("p t h d -> p t (h d)")

        w1 = f1[:, 0:FW].rearrange("p (x f) -> p x f", x=X)
        w2 = f1[:, FW:2 * FW].rearrange("p (x c h) -> p x c h", x=X, c=FC)
        gates = [(f0, f2)[i // 2][:, (i % 2) * X * QB:(i % 2 + 1) * X * QB].rearrange("p (x q) -> p x q", x=X)
                 for i in range(NB)]
        o1 = 2 * FW
        b1v = f1[:, o1:o1 + X * FC].rearrange("p (x c) -> p x c", x=X)
        wrv = f1[:, o1 + 32:o1 + 40]
        brv = f1[:, o1 + 40:o1 + 48]
        b2v = f1[0:X, o1 + 48:o1 + 48 + E]
        tiev = f1[:, o1 + 256:o1 + 320].rearrange("p (a b) -> p a b", a=X)
        lg = f1[:, o1 + 320:o1 + 448].rearrange("p (t x) -> p t x", x=X)
        gate = f1[:, o1 + 448:o1 + 576].rearrange("p (t x) -> p t x", x=X)
        rt1 = f1[:, o1 + 576:o1 + 592]
        rt2 = f1[:, o1 + 592:o1 + 608]
        cum = f1[:, o1 + 608:o1 + 736].rearrange("p (t x) -> p t x", x=X)
        eq0 = f1[:, o1 + 736:o1 + 864].rearrange("p (t x) -> p t x", x=X)
        oz = 2 * X * QB
        big1 = f0[:, oz:oz + T * X * X].rearrange("p (t a b) -> p t a b", a=X, b=X)
        big2 = f2[:, oz:oz + T * X * X].rearrange("p (t a b) -> p t a b", a=X, b=X)
        gateT = xn[:].rearrange("p t e -> p (t e)")
        hT = [xs[:, i, :] for i in range(4)]
        up = [parts[:, 0, 0:2, :].rearrange("p v q -> p (v q)").bitcast(F32),
              parts[:, 0, 2:4, :].rearrange("p v q -> p (v q)").bitcast(F32),
              parts[:, 1, 0:2, :].rearrange("p v q -> p (v q)").bitcast(F32)]
        yT = probs

        block = ctx.enter_context(nc.Block())

        @block.sync
        def _(sp):
            for i in range(NB):
                sp.dma_start(x[:, BT * i:BT * (i + 1), :],
                             a["x"][QB * i:QB * (i + 1), :].rearrange("(t p) e -> p t e", p=P)).then_inc(in_x[i], 16)
            for dst, name in ((ident, "c_ident"), (cols, "c_cols"), (dec, "dec"), (mixw, "mix"), (bqk, "bqk"),
                              (wqk, "wqk"), (wv, "wv"), (bvo, "bvo"), (absd, "c_absd"), (dist, "c_dist"),
                              (wo, "wo")):
                src = a[name]
                sp.dma_start(dst[:], src).then_inc(in_c, 16)
            for s in range(3):
                sp.dma_start(stage[s][KR:SH, 1, :, :], a["c_ones"]).then_inc(in_c, 16)

            def gather(it, k):
                s = k % U
                sp.wait_ge(parts_ready, count(it, 2, 2 * (k + 1)))
                for side in range(2):
                    for c, pair in enumerate(PAIRS):
                        for i in range(NB):
                            p0 = 2 * ROWS * i + ROWS * side
                            sp.dma_start(stage[s][ROWS * c:ROWS * (c + 1), side, :, QB * i:QB * (i + 1)],
                                         parts[p0:p0 + ROWS, pair[side], :, :]).then_inc(staged[s], 16)

            def maxima_rows(it, k):
                s = k % U
                sp.wait_ge(nmT_ready, count(it, 1, k + 1))
                apart(sp)
                for part in range(3):
                    for v in range(V):
                        sp.dma_start(
                            stage[s][KR + part:KR + part + 1, 0, v, :].rearrange("o (t q) -> o t q", q=P),
                            nmT[T * part:T * (part + 1), :]).then_inc(shifted[s], 16)

            for h in range(U):
                gather(None, h)
            maxima_rows(None, 0)

            def step(it, k):
                if it is not None or k + 1 < H:
                    maxima_rows(it, k + 1)
                sp.wait_ge(exp_done, count(it, UNITS, UNITS * (k + 1) + BSLOTS))
                apart(sp)
                if it is not None or k + U < H:
                    gather(it, k + U)
            steps(sp, step)

            sp.wait_ge(mask_ready, 2 * H)
            sp.dma_start(x1, a["x"].rearrange("(t p) e -> p t e", p=P)).then_inc(x1_in, 16)
            sp.dma_start(w1, a["w1"]).then_inc(w1_in, 16)
            sp.dma_start(w2, a["w2"]).then_inc(w2_in, 16)
            sp.dma_start(b1v, a["b1"]).then_inc(w1_in, 16)
            sp.dma_start(wrv, a["wr"]).then_inc(w1_in, 16)
            sp.dma_start(brv, a["br"]).then_inc(w1_in, 16)
            sp.dma_start(b2v, a["b2"]).then_inc(w1_in, 16)
            sp.dma_start(tiev, a["c_tie"]).then_inc(w1_in, 16)
            sp.wait_ge(gT_ready, 4)
            sp.dma_start(a["scratch"], gateT[0:X, :]).then_inc(g_out, 16)
            sp.wait_ge(g_out, 16)
            for i in range(NB):
                sp.dma_start(gates[i], a["scratch"][:, QB * i:QB * (i + 1)].unsqueeze(0)
                             .broadcast_to([P, X, QB])).then_inc(g_in, 16)
            for i in range(NB):
                sp.wait_ge(y_done, i + 1)
                sp.dma_start(out[QB * i:QB * (i + 1), :].rearrange("(t p) e -> p t e", p=P),
                             x1[:, BT * i:BT * (i + 1), :]).then_inc(stored, 16)
            sp.wait_ge(stored, 16 * NB)

        @block.gpsimd
        def _(pool):
            pool.memset(vh[:], 0.0).then_inc(ones_set, 1)
            pool.wait_ge(ones_set, 1)
            pool.memset(vh[:, :, :, D:D + 1], 1.0).then_inc(ones_set, 1)
            pool.sem_inc(o_ready, 1)
            pool.wait_ge(in_c, n_consts)
            pool.wait_ge(tables, 1)
            pool.wait_ge(v_ready, NB)

            def build(it, k):
                hd = head(it, k)
                done = [0]

                def link(ins):
                    done[0] += 1
                    ins.then_inc(pool_chain, 1)
                    pool.wait_ge(pool_chain, count(it, 8, 8 * k + done[0]))

                if it is not None or k >= 1:
                    pool.wait_ge(base_made, count(it, 1, k))
                apart(pool)
                pool.tensor_copy(wst[:], wqk[:, bass.ds(hd, 1), :]).then_inc(wst_ready, 1)
                pool.wait_ge(base_ready, count(it, 1, k + 1))
                link(pool.tensor_copy(mixh[:], mixt[:, bass.ds(hd, 1), :]))
                apart(pool)
                link(pool.tensor_scalar(basem[:], base[:], mixh[:, 0:1], None, ALU.mult))
                if it is not None or k >= 1:
                    pool.wait_ge(parts_ready, count(it, 2, 2 * k))
                apart(pool)
                pool.tensor_scalar(xs[:, V - 1, :], base[:], cols[:, 2:3], None, ALU.mult).then_inc(xs_ready, 1)
                for v in range(LV):
                    pool.wait_ge(fac_ready, count(it, LV, LV * k + v + 1))
                    pool.tensor_tensor(xs[:, v, :], xs[:, v, :], basem[:], ALU.mult).then_inc(xs_ready, 1)
                pool.wait_ge(high_ready, count(it, V, V * (k + 1)))
                halves = (slice(0, 2), slice(2, V))
                for vs in halves:
                    link(pool.tensor_tensor(xs[:, vs], xs[:, vs], parts[:, 0, vs], ALU.subtract))
                for vs in halves:
                    apart(pool)
                    link(pool.tensor_copy(parts[:, 1, vs], xs[:, vs]))
                for vs in halves:
                    pool.tensor_tensor(parts[:, 2, vs], xs[:, vs], parts[:, 1, vs], ALU.subtract)\
                        .then_inc(parts_ready, 1)
                pool.wait_ge(maske_ready, count(it, 1, k + 1))
                for n in range(N):
                    apart(pool)
                    link(pool.tensor_scalar(maske[:, n, :], maske[:, n, :], mixh[:, n + 1:n + 2], None, ALU.mult))
                if it is not None or k >= U:
                    pool.wait_ge(pv_used, count(it, UNITS, UNITS * (k - U + 1) + PSLOTS))
                pool.tensor_tensor(masks[:, k % U, :], maske[:, 0, :], maske[:, 1, :], ALU.add).then_inc(mask_ready, 1)
                pool.tensor_copy(vh[:, k % U, :, 0:D], x1[:, :, bass.ds(hd * D, D)]).then_inc(mask_ready, 1)

            for h in range(U):
                build(None, h)

            def output(it, k):
                hd = head(it, k)
                pool.wait_ge(rz_ready, count(it, 1, k + 1))
                pool.tensor_tensor(
                    xn[:, :, bass.ds(hd * D, D)], ou[:, :, 0:D],
                    widen(rz[:], D), ALU.mult).then_inc(o_ready, 1)

            def step(it, k):
                if it is not None or k + U < H:
                    build(it, k + U)
                output(it, k)
            steps(pool, step)

        @block.scalar
        def _(act):
            act.sem_inc(exp_done, BSLOTS)
            act.sem_inc(pv_out, 1)
            act.wait_ge(small, 2)
            act.activation(dec[:], dec[:], ACT.Ln).then_inc(small_act, 1)
            act.wait_ge(small, 4)
            act.activation(mixw[:], mixw[:], ACT.Exp).then_inc(small_act, 1)
            act.wait_ge(bn_done, 2 * T)
            act.activation(rstd[:], mv[:, :, 1], ACT.Sqrt, bias=cols[:, 4:5]).then_inc(sqrt_done, 1)
            for g in range(NB):
                act.wait_ge(transposed, g + 1)
                act.activation(xT[:, QB * g:QB * (g + 1)], (MISC, PV)[g % 2][:, :], ACT.Copy).then_inc(xT_ready, 1)
            act.wait_ge(tables, 1)

            def build(it, k):
                hd = head(it, k)
                act.wait_ge(base_made, count(it, 1, k + 1))
                if it is not None or k >= 1:
                    act.wait_ge(xs_ready, count(it, V, V * k))
                act.activation(base[:], MISC[:, :], ACT.Identity, bias=bqk[:, bass.ds(hd, 1)],
                               scale=cols[:, 0:1]).then_inc(base_ready, 1)

            def factor(it, k, v):
                if v == 0 and (it is not None or k >= 1):
                    act.wait_ge(parts_ready, count(it, 2, 2 * k))
                act.activation(xs[:, v, :], dist[:, QB * v:QB * (v + 1)], ACT.Exp,
                               scale=dec[:, bass.ds(head(it, k), 1)]).then_inc(fac_ready, 1)

            def high(it, k, v):
                order = (V - 1,) + tuple(range(LV))
                act.wait_ge(xs_ready, count(it, V, V * k + v + 1))
                if v == 0 and (it is not None or k >= 1):
                    act.wait_ge(staged[(k - 1) % U], gathered(it, k - 1))
                act.activation(parts[:, 0, order[v], :], xs[:, order[v], :], ACT.Copy).then_inc(high_ready, 1)

            def powers(it, k):
                if it is not None or k >= 1:
                    act.wait_ge(mask_ready, count(it, 2, 2 * k))
                act.activation(maske[:, 0, :], absd[:], ACT.Exp, scale=dec[:, bass.ds(head(it, k) * 2 + H, 1)])
                act.activation(maske[:, 1, :], absd[:], ACT.Exp,
                               scale=dec[:, bass.ds(head(it, k) * 2 + (H + 1), 1)]).then_inc(maske_ready, 1)

            for h in range(U):
                build(None, h)
                for v in range(LV):
                    factor(None, h, v)
                for v in range(V):
                    high(None, h, v)
                powers(None, h)

            def step(it, k):
                plain = diag = 0
                builds = it is not None or k + U < H
                for n in range(UNITS):
                    i, r = divmod(n, T)
                    j = key_order(i)[r]
                    if j // BT == i:
                        diag += 1
                        act.wait_ge(b_diag, count(it, T, k * T + diag))
                    else:
                        plain += 1
                        act.wait_ge(b_plain, count(it, UNITS - T, k * (UNITS - T) + plain))
                    act.wait_ge(pv_used, count(it, UNITS, k * UNITS + n + 1))
                    act.activation(probs[:, n % PSLOTS, :], SB[(k * UNITS + n) % BSLOTS][:, :], ACT.Exp)\
                       .then_inc(exp_done, 1)
                    if n >= T + LAG - 1 and (n - LAG + 1) % T == 0:
                        evacuate(it, k, (n - LAG + 1) // T - 1)
                    if builds:
                        if n == 8:
                            build(it, k + U)
                        if n in (10, 12, 14, 16):
                            factor(it, k + U, (n - 10) // 2)
                        if n in (22, 26, 30, 34, 38):
                            high(it, k + U, (n - 22) // 4)
                        if n == 56:
                            powers(it, k + U)
                evacuate(it, k, NB - 1)

            def evacuate(it, k, i):
                act.wait_ge(pv_used, count(it, UNITS, k * UNITS + T * (i + 1) + PSLOTS))
                act.wait_ge(pvs_free, count(it, NB, k * NB + i + 1))
                act.activation(pvs[:, i % 2, :], PV[:, :], ACT.Copy).then_inc(pv_out, 1)

            steps(act, step)

            for g in range(NB):
                act.wait_ge(oT_made, g + 1)
                act.activation(xT[:, QB * g:QB * (g + 1)], SA[g % 2][:, :], ACT.Copy).then_inc(oT_ready, 1)
            act.wait_ge(bn_done, 4 * T)
            act.activation(rstd[:], mv[:, :, 1], ACT.Sqrt, bias=cols[:, 4:5]).then_inc(sqrt_done, 1)
            for g in range(NB):
                act.wait_ge(transposed, NB + g + 1)
                act.activation(xT[:, QB * g:QB * (g + 1)], SA[g % 2][:, :], ACT.Copy).then_inc(xT_ready, 1)
            act.wait_ge(rt_step, 2)
            act.activation(lg[:], lg[:], ACT.Exp).then_inc(rt_act, 1)
            for g in range(NB):
                act.wait_ge(gT_made, g + 1)
                act.activation(gateT[0:X, QB * g:QB * (g + 1)], SB[g % 2][0:X, :], ACT.Copy).then_inc(gT_ready, 1)
            for i in range(NB):
                for u in range(X * FC):
                    g = i * X * FC + u
                    act.wait_ge(up_scaled, g + 1)
                    if g >= 4:
                        act.wait_ge(h_free, g - 3)
                    act.activation(hT[g % 4], up[g % 3], ACT.Relu).then_inc(h_ready, 1)
                act.wait_ge(h_free, X * FC * (i + 1))
                act.activation(yT[:, i, :], (PV, MISC)[i % 2][:, :], ACT.Copy).then_inc(y_out, 1)

        @block.tensor
        def _(pe):
            pe.sem_inc(pv_used, PSLOTS)
            pe.sem_inc(pvs_free, 2)
            pe.wait_ge(in_c, n_consts)
            for g in range(NB):
                pe.wait_ge(normed, BT * (g + 1))
                if g >= 2:
                    pe.wait_ge(xT_ready, g - 1)
                for t in range(BT):
                    mm = pe.transpose((MISC, PV)[g % 2][:, P * t:P * (t + 1)], xn[:, BT * g + t, :], ident[:])
                mm.then_inc(transposed, 1)
            for g in range(NB):
                pe.wait_ge(xT_ready, g + 1)
                for t in range(BT):
                    c = BT * g + t
                    mm = pe.matmul((SA[0], SA[1], SA[2], SB[0])[g][:, P * t:P * (t + 1)], xT[:, P * c:P * (c + 1)],
                                   wv[:], start=True, stop=True, skip_group_check=True)
                mm.then_inc(v_made, 1)

            def base_product(it, k):
                pe.wait_ge(wst_ready, count(it, 1, k + 1))
                for i in range(NB):
                    mm = pe.matmul(MISC[32 * i:32 * (i + 1), :], wst[:], xT[:, QB * i:QB * (i + 1)],
                                   start=True, stop=True, skip_group_check=True)
                mm.then_inc(base_made, 1)

            pe.wait_ge(xT_ready, NB)
            for h in range(U):
                if h:
                    pe.wait_ge(base_ready, h)
                base_product(None, h)

            def a_unit(it, k, n):
                i, b = divmod(n, NB)
                s = k % U
                g = (k * UNITS + n)
                pe.wait_ge(a_free, count(it, UNITS, g + 1))
                bank = SA[g % ASLOTS]
                for v, c0, cn in block_pieces(i // BT, b, i):
                    mm = pe.matmul(bank[:, c0:c0 + cn], stage[s][0:KR, 0, v, P * i:P * (i + 1)],
                                   stage[s][0:KR, 1, v, QB * b + c0:QB * b + c0 + cn],
                                   start=True, stop=True, skip_group_check=True)
                mm.then_inc(a_made, 1)

            def maxima(it, k):
                pe.wait_ge(nm_step, count(it, 5, 5 * (k + 1)))
                apart(pe)
                pe.transpose(MISC[:, :].bitcast(BF16)[0:3 * T, 0:P], nmp[:].rearrange("p a t -> p (a t)"), identb[:])\
                  .then_inc(nmT_made, 1)

            pe.wait_ge(staged[0], gathered(None, 0))
            for n in range(UNITS):
                a_unit(None, 0, n)
            pe.wait_ge(base_ready, U)
            maxima(None, 0)
            pe.wait_ge(staged[1], gathered(None, 1))
            for n in range(AHEAD):
                a_unit(None, 1, n)

            def step(it, k):
                s = k % U
                diag = [0]
                pe.wait_ge(shifted[s], shifts(it, k))
                for what, n in timeline(it, k):
                    i, r = divmod(n, T)
                    if what == "b":
                        j = key_order(i)[r]
                        g = k * UNITS + n
                        pe.wait_ge(exp_done, count(it, UNITS, g + 1))
                        bank = SB[g % BSLOTS]
                        for v, c0, cn in block_pieces(j // BT, i, j):
                            rows = KR if v == V - 1 else SH
                            mm = pe.matmul(bank[:, c0:c0 + cn], stage[s][0:rows, 1, v, P * j:P * (j + 1)],
                                           stage[s][0:rows, 0, v, QB * i + c0:QB * i + c0 + cn],
                                           start=True, stop=True, skip_group_check=True)
                        mm.then_inc(b_raw if j // BT == i else b_plain, 1)
                    elif what == "shift":
                        j = key_order(i)[r]
                        if j // BT != i:
                            continue
                        diag[0] += 1
                        pe.wait_ge(b_masked, count(it, T, k * T + diag[0]))
                        c0 = P * (j % BT)
                        pe.matmul(SB[(k * UNITS + n) % BSLOTS][:, c0:c0 + P], stage[s][KR:SH, 1, 0, 0:P],
                                  stage[s][KR:SH, 0, 0, P * j:P * (j + 1)], start=False, stop=True,
                                  skip_group_check=True).then_inc(b_diag, 1)
                    elif what == "a":
                        m = n + AHEAD
                        if m == UNITS:
                            pe.wait_ge(staged[(k + 2) % U], gathered(it, k + 2))
                        a_unit(it, k + 1 + m // UNITS, m % UNITS)
                    elif what == "maxima":
                        pe.wait_ge(ou_step, count(it, NB, NB * k + NB))
                        maxima(it, k + 1)
                    elif what == "base":
                        pe.wait_ge(ou_step, count(it, NB, NB * k + 1))
                        pe.wait_ge(nmT_ready, count(it, 1, k + 1))
                        base_product(it, k + U)
                    elif what == "pv":
                        if n == 0:
                            pe.wait_ge(mask_ready, count(it, 2, 2 * (k + 1)))
                        if n >= UNITS - LAG:
                            pe.wait_ge(exp_done, count(it, UNITS, k * UNITS + n + 1 + BSLOTS))
                        if r == 0:
                            pe.wait_ge(pv_out, count(it, NB, k * NB + i + 1))
                        j = key_order(i)[r]
                        c = r % 4
                        pe.matmul(PV[32 * c:32 * (c + 1), :], vh[:, s, j, :], probs[:, n % PSLOTS, :],
                                  start=(r < 4), stop=(r >= T - 4), skip_group_check=True).then_inc(pv_used, 1)
                    elif what == "sum":
                        i = n
                        pe.wait_ge(pv_out, count(it, NB, k * NB + i + 2))
                        pe.wait_ge(ou_step, count(it, NB, NB * k + i + 1))
                        if i == 0 and (it is not None or k + U < H):
                            pe.wait_ge(base_ready, count(it, 1, k + U + 1))
                        if i == NB - 1 and (it is not None or k + 1 < H):
                            pe.wait_ge(nmT_ready, count(it, 1, k + 2))
                        for t in range(BT):
                            mm = pe.transpose(MISC[:, P * t:P * (t + 1)], pvs[:, i % 2, P * t:P * (t + 1)], ident[:])
                        mm.then_inc(pvs_free, 1)
            steps(pe, step)

            pe.wait_ge(o_ready, H + 1)
            for g in range(NB):
                if g >= 2:
                    pe.wait_ge(oT_ready, g - 1)
                for t in range(BT):
                    mm = pe.transpose(SA[g % 2][:, P * t:P * (t + 1)], xn[:, BT * g + t, :], ident[:])
                mm.then_inc(oT_made, 1)
            for g in range(NB):
                pe.wait_ge(oT_ready, g + 1)
                if g >= 2:
                    pe.wait_ge(x1_ready, g)
                for t in range(BT):
                    c = BT * g + t
                    mm = pe.matmul(SB[g % 2][:, P * t:P * (t + 1)], xT[:, P * c:P * (c + 1)], wo[:],
                                   start=True, stop=True, skip_group_check=True)
                mm.then_inc(wo_made, 1)
            for g in range(NB):
                pe.wait_ge(normed, T + BT * (g + 1))
                if g >= 2:
                    pe.wait_ge(xT_ready, NB + g - 1)
                for t in range(BT):
                    mm = pe.transpose(SA[g % 2][:, P * t:P * (t + 1)], xn[:, BT * g + t, :], ident[:])
                mm.then_inc(transposed, 1)
            pe.wait_ge(xT_ready, 2 * NB)
            pe.wait_ge(w1_in, 16 * 6)
            for t in range(T):
                mm = pe.matmul(SA[2][:, X * t:X * (t + 1)], xT[:, P * t:P * (t + 1)], wrv,
                               start=True, stop=True, skip_group_check=True)
            mm.then_inc(rt_made, 1)
            pe.wait_ge(rt_step, RT_STEPS)
            for g in range(NB):
                if g >= 2:
                    pe.wait_ge(gT_ready, g - 1)
                for t in range(BT):
                    mm = pe.transpose(SB[g % 2][0:X, P * t:P * (t + 1)], gate[:, BT * g + t, :], ident[:])
                mm.then_inc(gT_made, 1)
            pe.wait_ge(w2_in, 16)
            total = NB * X * FC

            def up_product(g):
                i, u = divmod(g, X * FC)
                e, c = divmod(u, FC)
                if g >= 3:
                    pe.wait_ge(up_scaled, g - 2)
                pe.matmul(SA[g % 3][:, :], w1[:, e, P * c:P * (c + 1)], xT[:, QB * i:QB * (i + 1)],
                          start=True, stop=True, skip_group_check=True).then_inc(up_made, 1)

            def down_product(g):
                i, u = divmod(g, X * FC)
                e, c = divmod(u, FC)
                bank = (PV, MISC)[i % 2]
                if u == 0:
                    if i >= 2:
                        pe.wait_ge(y_out, i - 1)
                    pe.wait_ge(gT_ready, NB)
                    pe.matmul(bank[:, :], b2v, gateT[0:X, QB * i:QB * (i + 1)], start=True, stop=False,
                              skip_group_check=True)
                pe.wait_ge(h_ready, g + 1)
                mm = pe.matmul(bank[:, :], w2[:, e, c, :], hT[g % 4], start=False, stop=(u == X * FC - 1),
                               skip_group_check=True)
                mm.then_inc(h_free, 1)

            def y_transposes(i):
                pe.wait_ge(y_out, i + 1)
                if i >= 2:
                    pe.wait_ge(y_done, i - 1)
                for t in range(BT):
                    mm = pe.transpose(SB[i % 2][:, P * t:P * (t + 1)], yT[:, i, P * t:P * (t + 1)], ident[:])
                mm.then_inc(yT_made, 1)

            for g in range(total + 2):
                if g < total:
                    up_product(g)
                if g >= 2:
                    down_product(g - 2)
                    if (g - 2) % (X * FC) == 4 and g > X * FC:
                        y_transposes((g - 2) // (X * FC) - 1)
            y_transposes(NB - 1)

        @block.vector
        def _(dve):
            dve.sem_inc(a_free, ASLOTS)
            dve.sem_inc(ou_step, 1)

            def step_of(s, count, ins):
                count[0] += 1
                ins.then_inc(s, 1)
                dve.wait_ge(s, count[0])

            dve.wait_ge(in_c, n_consts)
            dve.tensor_copy(identb[:], ident[:])
            sm = [0]
            step_of(small, sm, dve.tensor_scalar(dec[:], dec[:], 0.01, 0.9999, ALU.max, ALU.min))
            step_of(small, sm, dve.tensor_tensor(mixs[:, 0, :], mixw[:, :, 0], mixw[:, :, 1], ALU.max))
            for n in range(N):
                step_of(small, sm, dve.tensor_tensor(mixw[:, :, n], mixw[:, :, n], mixs[:, 0, :], ALU.subtract))
            dve.wait_ge(small_act, 2)
            step_of(small, sm, dve.tensor_tensor(mixs[:, 0, :], mixw[:, :, 0], mixw[:, :, 1], ALU.add))
            step_of(small, sm, dve.reciprocal(mixs[:, 1, :], mixs[:, 0, :]))
            for n in range(N):
                step_of(small, sm, dve.tensor_tensor(mixt[:, :, 1 + n], mixw[:, :, n], mixs[:, 1, :], ALU.mult))
            step_of(small, sm, dve.tensor_scalar(mixs[:, 2, :], mixt[:, :, 1], cols[:, 5:6], cols[:, 1:2],
                                                 ALU.mult, ALU.add))
            step_of(small, sm, dve.scalar_tensor_tensor(mixt[:, :, 0], mixt[:, :, 2], cols[:, 6:7], mixs[:, 2, :],
                                                        ALU.mult, ALU.add))
            step_of(small, sm, dve.tensor_scalar(bqk[:], bqk[:], cols[:, 0:1], None, ALU.mult))
            dve.sem_inc(tables, 1)

            def layer_norm(src, part):
                for t in range(T):
                    if part == 0:
                        dve.wait_ge(in_x[t // BT], 16)
                    dve.bn_stats(stats[:, t, :], src[:, t, :]).then_inc(bn_done, 1)
                dve.wait_ge(bn_done, 2 * T * part + T)
                for t in range(T):
                    dve.bn_aggr(mv[:, t, :], stats[:, t, :]).then_inc(bn_done, 1)
                dve.wait_ge(sqrt_done, part + 1)
                dve.reciprocal(rstd[:], rstd[:]).then_inc(rstd_ready, 1)
                dve.wait_ge(rstd_ready, part + 1)
                for t in range(T):
                    dve.tensor_scalar(xn[:, t, :], src[:, t, :], mv[:, t, 0:1], rstd[:, t:t + 1],
                                      ALU.subtract, ALU.mult).then_inc(normed, 1)

            layer_norm(x, 0)
            for g in range(NB):
                dve.wait_ge(v_made, g + 1)
                bank = (SA[0], SA[1], SA[2], SB[0])[g]
                for t in range(BT):
                    ins = dve.tensor_tensor(vals[:, BT * g + t, :, :].rearrange("p h d -> p (h d)"),
                                            bank[:, P * t:P * (t + 1)], bvo[:, 0, :], ALU.add)
                ins.then_inc(v_ready, 1)

            def a_max(it, k, n):
                i, b = divmod(n, NB)
                g = k * UNITS + n
                bank = SA[g % ASLOTS]
                dve.wait_ge(a_made, count(it, UNITS, g + 1))
                if b == i // BT:
                    if n == 0:
                        dve.wait_ge(mask_ready, count(it, 2, 2 * (k + 1)))
                    c0 = P * (i % BT)
                    dve.tensor_tensor(bank[:, c0:c0 + P], bank[:, c0:c0 + P], masks[:, k % U, :], ALU.mult)\
                       .then_inc(a_masked, 1)
                    dve.wait_ge(a_masked, count(it, T, k * T + i + 1))
                dve.tensor_reduce(mx[:, n:n + 1], bank[:, :], AX.X, ALU.max).then_inc(a_free, 1)

            def finish(it, k):
                c = [0]

                def link(ins):
                    c[0] += 1
                    ins.then_inc(nm_step, 1)
                    dve.wait_ge(nm_step, count(it, 5, 5 * k + c[0]))
                dve.wait_ge(a_free, count(it, UNITS, (k + 1) * UNITS + ASLOTS))
                link(dve.tensor_reduce(nm[:, 0, :], mx[:].rearrange("p (t b) -> p t b", b=NB), AX.X, ALU.max,
                                       negate=True))
                link(dve.tensor_copy(nmp[:, 0, :], nm[:, 0, :]))
                link(dve.tensor_tensor(nm[:, 1, :], nm[:, 0, :], nmp[:, 0, :], ALU.subtract))
                link(dve.tensor_copy(nmp[:, 1, :], nm[:, 1, :]))
                link(dve.tensor_tensor(nmp[:, 2, :], nm[:, 1, :], nmp[:, 1, :], ALU.subtract))

            def maxima_out(it, k):
                dve.wait_ge(nmT_made, count(it, 1, k + 1))
                if it is not None or k >= 1:
                    dve.wait_ge(shifted[(k - 1) % U], shifts(it, k - 1))
                dve.tensor_copy(nmT[:], MISC[:, :].bitcast(BF16)[0:3 * T, 0:P]).then_inc(nmT_ready, 1)

            def first_maxima():
                for n in range(UNITS):
                    a_max(None, 0, n)
                finish(None, 0)
                maxima_out(None, 0)
                for n in range(AHEAD):
                    a_max(None, 1, n)

            first_maxima()

            def step(it, k):
                diag = [0]
                for what, n in timeline(it, k):
                    i, r = divmod(n, T)
                    if what == "b":
                        j = key_order(i)[r]
                        if j // BT != i:
                            continue
                        diag[0] += 1
                        c0 = P * (j % BT)
                        tile = SB[(k * UNITS + n) % BSLOTS][:, c0:c0 + P]
                        dve.wait_ge(b_raw, count(it, T, k * T + diag[0]))
                        dve.tensor_tensor(tile, tile, masks[:, k % U, :], ALU.mult).then_inc(b_masked, 1)
                    elif what == "a":
                        m = n + AHEAD
                        a_max(it, k + 1 + m // UNITS, m % UNITS)
                        if m == UNITS - 1:
                            finish(it, k + 1)
                    elif what == "maxima":
                        maxima_out(it, k + 1)
                    elif what == "sum":
                        i = n
                        dve.wait_ge(pvs_free, count(it, NB, k * NB + i + 3))
                        if i == 0:
                            dve.wait_ge(o_ready, count(it, 1, k + 1))
                        dve.tensor_reduce(
                            ou[:, BT * i:BT * (i + 1), :],
                            MISC[:, :].rearrange("p (t c d) -> p t d c", t=BT, c=4)[:, :, 0:D + 1, :],
                            AX.X, ALU.add).then_inc(ou_step, 1)
                        if i == NB - 1:
                            dve.wait_ge(ou_step, count(it, NB, NB * (k + 1) + 1))
                            dve.reciprocal(rz[:], ou[:, :, D]).then_inc(rz_ready, 1)
            steps(dve, step)

            dve.wait_ge(x1_in, 16)
            dve.tensor_tensor(x1, x1, bvo[:, 1:2, :].broadcast_to([P, T, E]), ALU.add).then_inc(x1_ready, 1)
            dve.wait_ge(x1_ready, 1)
            for g in range(NB):
                dve.wait_ge(wo_made, g + 1)
                rows = x1[:, BT * g:BT * (g + 1), :]
                dve.tensor_tensor(rows, rows, SB[g % 2][:, :].rearrange("p (t e) -> p t e", e=E), ALU.add)\
                   .then_inc(x1_ready, 1)
            dve.wait_ge(x1_ready, NB + 1)
            layer_norm(x1, 1)

            c = [0]

            def link(ins):
                step_of(rt_step, c, ins)

            dve.wait_ge(rt_made, 1)
            dve.wait_ge(w1_in, 16 * 6)
            dve.tensor_tensor(lg[:], SA[2][:, 0:T * X].rearrange("p (t x) -> p t x", x=X),
                              brv.unsqueeze(1).broadcast_to([P, T, X]), ALU.add).then_inc(lg_ready, 1)
            dve.wait_ge(lg_ready, 1)
            link(dve.tensor_reduce(rt1, lg[:], AX.X, ALU.max))
            link(dve.tensor_tensor(lg[:], lg[:], widen(rt1, X), ALU.subtract))
            dve.wait_ge(rt_act, 1)
            link(dve.tensor_reduce(rt1, lg[:], AX.X, ALU.add))
            link(dve.reciprocal(rt2, rt1))
            link(dve.tensor_tensor(lg[:], lg[:], widen(rt2, X), ALU.mult))
            mine = lg.unsqueeze(3).broadcast_to([P, T, X, X])
            theirs = lg.unsqueeze(2).broadcast_to([P, T, X, X])
            tie = tiev.unsqueeze(1).broadcast_to([P, T, X, X])
            link(dve.tensor_tensor(big1, theirs, mine, ALU.is_equal))
            link(dve.tensor_tensor(big1, big1, tie, ALU.mult))
            link(dve.tensor_tensor(big2, theirs, mine, ALU.is_gt))
            link(dve.tensor_tensor(big1, big1, big2, ALU.add))
            link(dve.tensor_tensor(big1, big1, theirs, ALU.mult))
            link(dve.tensor_reduce(cum, big1, AX.X, ALU.add))
            link(dve.tensor_scalar(eq0, cum, 0.0, None, ALU.is_equal))
            link(dve.tensor_tensor(cum, cum, lg[:], ALU.add))
            link(dve.tensor_scalar(cum, cum, TOP_P, None, ALU.is_lt))
            link(dve.tensor_tensor(cum, cum, eq0, ALU.max))
            link(dve.tensor_tensor(gate, cum, lg[:], ALU.mult))

            def add_y(i):
                dve.wait_ge(yT_made, i + 1)
                rows = x1[:, BT * i:BT * (i + 1), :]
                dve.tensor_tensor(rows, rows, SB[i % 2][:, :].rearrange("p (t e) -> p t e", e=E), ALU.add)\
                   .then_inc(y_done, 1)

            for i in range(NB):
                dve.wait_ge(g_in, 16 * NB)
                for u in range(X * FC):
                    g = i * X * FC + u
                    e, c2 = divmod(u, FC)
                    dve.wait_ge(up_made, g + 1)
                    if g >= 3:
                        dve.wait_ge(h_ready, g - 2)
                    dve.scalar_tensor_tensor(up[g % 3], SA[g % 3][:, :], b1v[:, e, c2:c2 + 1], gates[i][:, e, :],
                                             ALU.add, ALU.mult).then_inc(up_scaled, 1)
                    if i >= 1 and u == 8:
                        add_y(i - 1)
            add_y(NB - 1)



RT_STEPS = 16


def kernel(**inputs):
    import concourse.bacc as _bacc
    from concourse.bass_utils import run_bass_kernel_spmd as _run

    g = {k.split("_", 1)[1]: np.asarray(v) for k, v in inputs.items()}

    def everywhere(v):
        return np.broadcast_to(v, (P,) + v.shape)

    def qk_rows(q, k):
        q, k = (np.repeat(m.reshape(H, 1, D, -1), N, 1) for m in (q, k))
        return np.stack([q, k], 1).reshape(H, 2 * ROWS, -1)

    wqk = qk_rows(g["attn_Wq"], g["attn_Wk"]).transpose(2, 0, 1)
    bqk = np.tile(qk_rows(g["attn_bq"], g["attn_bk"])[:, :, 0].T, (NB, 1))
    dec = g["attn_decay_params"]
    by_row = np.tile(np.repeat(dec.T, D, 0), (2 * NB, 1))
    token = np.arange(S).reshape(NB, 1, QB)
    dist = np.stack([np.abs(token % (2 * w) - w) for w in WIDTHS], 1).reshape(NB, 1, LV * QB)
    lane = np.arange(P)
    query, second = lane // ROWS % 2 == 0, lane // D % 2 == 1
    cols = np.zeros((P, 8), np.float32)
    cols[:, 0] = np.where(query, D ** -0.5, 1)
    cols[:, 1] = ~query
    cols[:, 2] = np.where(query, 1 / N, 1)
    cols[:, 4] = EPS
    cols[:, 5] = query & ~second
    cols[:, 6] = query & second
    lower = np.arange(X)[None, :] < np.arange(X)[:, None]
    arrays = {
        "x": g["attn_x"].reshape(S, E),
        "wqk": wqk, "bqk": bqk, "wv": g["attn_Wv"].T, "wo": g["attn_Wo"].T,
        "bvo": everywhere(np.stack([g["attn_bv"], g["attn_bo"]])),
        "dec": np.concatenate([by_row, everywhere(dec.reshape(-1))], 1),
        "mix": everywhere(g["attn_mix_weights"]),
        "wr": g["ffn_Wr"], "br": everywhere(g["ffn_br"]),
        "w1": g["ffn_W1"].transpose(1, 0, 2),
        "b1": g["ffn_b1"].reshape(X, FC, P).transpose(2, 0, 1),
        "w2": g["ffn_W2"].reshape(X, FC, P, E).transpose(2, 0, 1, 3),
        "b2": g["ffn_b2"],
        "c_ident": np.eye(P, dtype=np.float32),
        "c_cols": cols,
        "c_dist": np.broadcast_to(dist, (NB, 2 * ROWS, LV * QB)).reshape(P, LV * QB).astype(np.float16),
        "c_absd": np.abs(lane[:, None] - lane[None, :]).astype(np.float32),
        "c_ones": np.ones((3, V, S), mybir.dt.np(BF16)),
        "c_tie": everywhere(lower.astype(np.float32)),
    }
    nc = _bacc.Bacc("TRN2", target_bir_lowering=False, num_devices=1)
    aps, feed = {}, {}
    for name, v in arrays.items():
        feed[f"in_{name}"] = np.ascontiguousarray(v)
        aps[name] = nc.dram_tensor(f"in_{name}", v.shape, mybir.dt.from_np(v.dtype), kind="ExternalInput").ap()
    aps["scratch"] = nc.dram_tensor("scratch", (X, S), F32, kind="Internal").ap()
    out = nc.dram_tensor("out", (S, E), F32, kind="ExternalOutput").ap()
    build_program(nc, aps, out)
    r = _run(nc, [feed], core_ids=[0])
    return r.results[0]["out"].reshape(1, S, E)
```

```python
from contextlib import ExitStack

import numpy as np

import concourse.bass as bass
from concourse import mybir

ALU = mybir.AluOpType
ACT = mybir.ActivationFunctionType
AX = mybir.AxisListType
F32 = mybir.dt.float32
BF16 = mybir.dt.bfloat16
F16 = mybir.dt.float16

P = 128
S = 2048
E = 128
H, D, N = 16, 8, 2
T = S // P
QB = 512
NB = S // QB
BT = QB // P
X, F = 8, 512
FC = F // P
EPS = 1e-5
TOP_P = 0.8

WIDTHS = (1024, 512, 256, 128)
LV = len(WIDTHS)
V = LV + 1
ROWS = N * D
PAIRS = ((0, 0), (0, 1), (0, 2), (1, 0), (1, 1), (2, 0))
RUNS = ((0, 3), (3, 2), (5, 1))
KR = len(PAIRS) * ROWS
SH = KR + 3

ASLOTS, BSLOTS, PSLOTS = 3, 3, 6
U = 3
STEPS_IN_LOOP = 12
GROUP = 4
LAG = 3
EARLY = 1
AHEAD = 20
BUILD_ORDER = (V - 1,) + tuple(range(LV))
POOL_LINKS = 2 + N
UNITS = T * NB
BUILD_TICKS = (("base", (15,)), ("factor", (17, 21, 23, 25)), ("high", (27, 29, 31, 37, 39)),
               ("middle", (41, 43, 45, 47, 53)), ("powers", (59,)))
MAXIMA_SUMS = 2


def block_pieces(own, other, tile):
    if own != other:
        v = 0 if own // 2 != other // 2 else 1
        return [(v, 0, QB)]
    a = tile % BT
    return [(2, 256 * (1 - a // 2), 256), (3, 128 * (a ^ 1), 128), (V - 1, 128 * a, 128)]


def key_order(block):
    diag = [BT * block + a for a in range(BT)]
    rest = [j for j in range(T) if j // BT != block]
    out = []
    for a in range(BT):
        out += [diag[a]] + rest[3 * a:3 * a + 3]
    return out


def diagonals(n):
    return sum(key_order(u // T)[u % T] // BT == u // T for u in range(n))


def build_program(nc, a, out):
    ctx = ExitStack()
    with ctx:
        def sb(name, shape, dt=F32):
            return ctx.enter_context(nc.sbuf_tensor(name, shape, dt))

        def sem(name):
            return ctx.enter_context(nc.semaphore(name))

        xn = sb("xn", [P, T, E])
        xT = sb("xT", [P, S])
        ident = sb("ident", [P, P])
        identb = sb("identb", [P, P], BF16)
        dist = sb("dist", [P, LV * QB], F16)
        absd = sb("absd", [P, P])
        groups = sb("groups", [P, D + 1])
        cols = sb("cols", [P, 8])
        wqk = sb("wqk", [P, H, 2 * ROWS])
        wv = sb("wv", [P, E])
        wo = sb("wo", [P, E])
        bvo = sb("bvo", [P, 2, E])
        bqk = sb("bqk", [P, H])
        dec = sb("dec", [P, H + 2 * H])
        mixw = sb("mixw", [P, H, N])
        mixs = sb("mixs", [P, 3, H])
        mixt = sb("mixt", [P, H, 1 + N])
        mixh = sb("mixh", [P, 1 + N])
        stats = sb("stats", [P, T, 6])
        mv = sb("mv", [P, T, 2])
        rstd = sb("rstd", [P, T])
        wst = sb("wst", [P, 2 * ROWS])
        base = sb("base", [P, QB])
        xs = sb("xs", [P, V, QB])
        parts = sb("parts", [P, 3, V, QB], BF16)
        stage = [sb(f"stage{s}", [P, 2, NB, V, QB], BF16) for s in range(U)]
        masks = sb("masks", [P, U, P])
        maske = sb("maske", [P, 2, P])
        vals = sb("vals", [P, T, H, D])
        vh = sb("vh", [P, U, T, 32])
        probs = sb("probs", [P, PSLOTS, QB])
        pvs = sb("pvs", [P, 2, QB])
        mx = sb("mx", [P, T * NB])
        nm = sb("nm", [P, 2, T])
        nmp = sb("nmp", [P, NB, 3, BT], BF16)
        nmT = sb("nmT", [3 * T, P], BF16)
        ou = sb("ou", [P, T, D + 1])
        rz = sb("rz", [P, T])

        SA = [ctx.enter_context(nc.psum_tensor(f"SA{i}", [P, QB], F32)) for i in range(ASLOTS)]
        SB = [ctx.enter_context(nc.psum_tensor(f"SB{i}", [P, QB], F32)) for i in range(BSLOTS)]
        PV = ctx.enter_context(nc.psum_tensor("PV", [P, QB], F32))
        MISC = ctx.enter_context(nc.psum_tensor("MISC", [P, QB], F32))

        in_x = [sem(f"in_x{i}") for i in range(NB)]
        in_c = sem("in_c")
        in_t = sem("in_t")
        in_rest = sem("in_rest")
        passed = sem("passed")
        ones_set = sem("ones_set")
        bn_done = sem("bn_done")
        rstd_ready = sem("rstd_ready")
        sqrt_done = sem("sqrt_done")
        normed = sem("normed")
        transposed = sem("transposed")
        xT_ready = sem("xT_ready")
        v_made = sem("v_made")
        v_ready = sem("v_ready")
        small = sem("small")
        small_act = sem("small_act")
        tables = sem("tables")

        wst_ready = sem("wst_ready")
        base_made = sem("base_made")
        base_ready = sem("base_ready")
        fac_ready = sem("fac_ready")
        maske_ready = sem("maske_ready")
        xs_ready = sem("xs_ready")
        high_ready = sem("high_ready")
        rest_ready = sem("rest_ready")
        middle_ready = sem("middle_ready")
        pool_chain = sem("pool_chain")
        parts_ready = sem("parts_ready")
        mask_ready = sem("mask_ready")
        staged = [sem(f"staged{s}") for s in range(U)]
        shifted = [sem(f"shifted{s}") for s in range(U)]

        a_made = sem("a_made")
        a_free = sem("a_free")
        a_masked = sem("a_masked")
        b_plain = sem("b_plain")
        b_raw = sem("b_raw")
        b_masked = sem("b_masked")
        b_diag = sem("b_diag")
        exp_done = sem("exp_done")
        pv_used = sem("pv_used")
        pv_out = sem("pv_out")
        pvs_free = sem("pvs_free")
        ou_step = sem("ou_step")
        rz_ready = sem("rz_ready")
        o_ready = sem("o_ready")
        nm_step = sem("nm_step")
        nmT_made = sem("nmT_made")
        nmT_ready = sem("nmT_ready")

        x1_in, small_in, w1_in, w2_in = sem("x1_in"), sem("small_in"), sem("w1_in"), sem("w2_in")
        oT_made, oT_ready = sem("oT_made"), sem("oT_ready")
        wo_made, x1_ready = sem("wo_made"), sem("x1_ready")
        x1_biased = sem("x1_biased")
        lg_ready = sem("lg_ready")
        rt_made, rt_step, rt_act = sem("rt_made"), sem("rt_step"), sem("rt_act")
        gT_made, gT_ready = sem("gT_made"), sem("gT_ready")
        g_out = sem("g_out")
        g_in = [sem(f"g_in{i}") for i in range(NB * 2)]
        up_made, up_scaled, h_ready = sem("up_made"), sem("up_scaled"), sem("h_ready")
        h_free = sem("h_free")
        y_out, yT_made, y_done, stored = sem("y_out"), sem("yT_made"), sem("y_done"), sem("stored")

        n_consts = 8 * 16

        class Turn:
            def __init__(self, eng, index, value):
                self.eng, self.index, self.value = eng, index, value

        def count_turns(it, per_turn, n):
            if it is None:
                return n
            it.eng.reg_add(it.value, it.index * per_turn, n)
            return it.value

        def count(it, per_head, n):
            return count_turns(it, U * per_head, n)

        def apart(eng):
            eng.sem_inc(passed, 1)

        def head(it, k):
            return k if it is None else it.index * U + k

        def gathered(it, k):
            n = 16 * 2 * len(RUNS) * NB
            return count_turns(it, n, (k // U + 1) * n)

        def shifts(it, k):
            n = 16 * LV * NB
            return count_turns(it, n, (k // U + 1) * n)

        def turns(eng, body):
            value = eng.alloc_register("wait_value")
            with eng.Fori(0, STEPS_IN_LOOP // U) as index:
                body(Turn(eng, index, value), range(U))
            body(None, range(STEPS_IN_LOOP, H))

        def builds(it, k):
            return it is not None or k + U < H

        def timeline(it, heads):
            units = [(k, n) for k in heads for n in range(UNITS)]
            seq = []
            for u in range(len(units) + LAG + 9):
                if u < len(units):
                    k, n = units[u]
                    m = n + AHEAD
                    ahead = it is not None or k + 1 + m // UNITS < H
                    seq.append(("b", k, n))
                if 1 <= u <= len(units):
                    seq.append(("shift",) + units[u - 1])
                if u < len(units):
                    if ahead:
                        seq.append(("a", k, n))
                    if n == UNITS - AHEAD + 3 and (it is not None or k + 1 < H):
                        seq.append(("maxima", k, 0))
                    if n == 12 and builds(it, k):
                        seq.append(("base", k, 0))
                if u >= LAG and u - LAG < len(units) and (u - LAG) % GROUP == GROUP - 1:
                    k, n = units[u - LAG]
                    seq.append(("pv", k, n // GROUP))
                w = u - LAG - 5
                if T <= w + 1 < len(units) + BT and (w + 1) % T < BT:
                    k, n = units[(w + 1) // T * T - 1]
                    seq.append(("sum", k, n // T * BT + (w + 1) % T))
            return seq

        def widen(ap, n):
            return ap.unsqueeze(2).broadcast_to([P, T, n])

        f0 = stage[0][:].rearrange("p a b v q -> p (a b v q)").bitcast(F32)
        f1 = stage[1][:].rearrange("p a b v q -> p (a b v q)").bitcast(F32)
        f2 = stage[2][:].rearrange("p a b v q -> p (a b v q)").bitcast(F32)
        FW = X * F
        x = f2[:, 0:T * E].rearrange("p (t e) -> p t e", e=E)
        x1 = vals[:].rearrange("p t h d -> p t (h d)")

        w1 = f1[:, 0:FW].rearrange("p (x f) -> p x f", x=X)
        w2 = f1[:, FW:2 * FW].rearrange("p (x c h) -> p x c h", x=X, c=FC)
        gates = [(f0, f2)[i // 2][:, (i % 2) * X * QB:(i % 2 + 1) * X * QB].rearrange("p (x q) -> p x q", x=X)
                 for i in range(NB)]
        o1 = 2 * FW
        b1v = f1[:, o1:o1 + X * FC].rearrange("p (x c) -> p x c", x=X)
        wrv = f1[:, o1 + 32:o1 + 40]
        brv = f1[:, o1 + 40:o1 + 48]
        b2v = f1[0:X, o1 + 48:o1 + 48 + E]
        tiev = f1[:, o1 + 256:o1 + 320].rearrange("p (a b) -> p a b", a=X)
        lg = f1[:, o1 + 320:o1 + 448].rearrange("p (t x) -> p t x", x=X)
        gate = f1[:, o1 + 448:o1 + 576].rearrange("p (t x) -> p t x", x=X)
        rt1 = f1[:, o1 + 576:o1 + 592]
        rt2 = f1[:, o1 + 592:o1 + 608]
        cum = f1[:, o1 + 608:o1 + 736].rearrange("p (t x) -> p t x", x=X)
        eq0 = f1[:, o1 + 736:o1 + 864].rearrange("p (t x) -> p t x", x=X)
        oz = 2 * X * QB
        big1 = f0[:, oz:oz + T * X * X].rearrange("p (t a b) -> p t a b", a=X, b=X)
        big2 = f2[:, oz:oz + T * X * X].rearrange("p (t a b) -> p t a b", a=X, b=X)
        gateT = xn[:].rearrange("p t e -> p (t e)")
        hT = [xs[:, i, :] for i in range(4)]
        up = [parts[:, 0, 0:2, :].rearrange("p v q -> p (v q)").bitcast(F32),
              parts[:, 0, 2:4, :].rearrange("p v q -> p (v q)").bitcast(F32),
              parts[:, 1, 0:2, :].rearrange("p v q -> p (v q)").bitcast(F32)]
        yT = probs

        block = ctx.enter_context(nc.Block())

        @block.sync
        def _(sp):
            for i in range(NB):
                sp.dma_start(x[:, BT * i:BT * (i + 1), :],
                             a["x"][QB * i:QB * (i + 1), :].rearrange("(t p) e -> p t e", p=P)).then_inc(in_x[i], 16)
            for dst, name in ((cols, "c_cols"), (dec, "dec"), (mixw, "mix"), (bqk, "bqk")):
                sp.dma_start(dst[:], a[name]).then_inc(in_t, 16)
            for dst, name in ((ident, "c_ident"), (wqk, "wqk"), (wv, "wv"), (bvo, "bvo"), (dist, "c_dist"),
                              (absd, "c_absd"), (groups, "c_groups"), (wo, "wo")):
                sp.dma_start(dst[:], a[name]).then_inc(in_c, 16)
            for s in range(U):
                sp.dma_start(stage[s][KR:P, 1], a["c_rest"]).then_inc(in_rest, 16)
            for s in range(U):
                if s == U - 1:
                    sp.wait_ge(normed, T)
                sp.dma_start(stage[s][SH:P, 0], a["c_rest"][SH - KR:]).then_inc(in_rest, 16)

            def gather(it, k):
                s = k % U
                sp.wait_ge(parts_ready, count(it, V, V * (k + 1)))
                for c, n in RUNS:
                    for side in range(2):
                        for i in range(NB):
                            p0 = 2 * ROWS * i + ROWS * side
                            src = parts[p0:p0 + ROWS, 0:n, :, :] if side else \
                                parts[p0:p0 + ROWS, PAIRS[c][0]:PAIRS[c][0] + 1, :, :].broadcast_to([ROWS, n, V, QB])
                            sp.dma_start(stage[s][ROWS * c:ROWS * (c + n), side, i, :, :],
                                         src).then_inc(staged[s], 16)

            def maxima_rows(it, k):
                s = k % U
                sp.wait_ge(nmT_ready, count(it, 1, k + 1))
                apart(sp)
                for i in range(NB):
                    for v in range(LV):
                        sp.dma_start(stage[s][KR:SH, 0, i, v, :], nmT[3 * BT * i:3 * BT * (i + 1), :])\
                            .then_inc(shifted[s], 16)

            for h in range(U):
                gather(None, h)
            maxima_rows(None, 0)

            def turn(it, heads):
                for k in heads:
                    if it is not None or k + 1 < H:
                        maxima_rows(it, k + 1)
                    sp.wait_ge(exp_done, count(it, UNITS, UNITS * (k + 1) + BSLOTS))
                    apart(sp)
                    if builds(it, k):
                        gather(it, k + U)
                    if it is None and k == H - U:
                        sp.wait_ge(mask_ready, 2 * H)
                        sp.dma_start(x1, a["x"].rearrange("(t p) e -> p t e", p=P)).then_inc(x1_in, 16)
                        for dst, name, s in ((wrv, "wr", small_in), (brv, "br", small_in), (b1v, "b1", small_in),
                                             (b2v, "b2", small_in), (tiev, "c_tie", small_in), (w1, "w1", w1_in),
                                             (w2, "w2", w2_in)):
                            sp.dma_start(dst, a[name]).then_inc(s, 16)
            turns(sp, turn)

            sp.wait_ge(gT_ready, 4)
            sp.dma_start(a["scratch"], gateT[0:X, :]).then_inc(g_out, 16)
            sp.wait_ge(g_out, 16)
            for i in range(NB):
                for part, (e0, e1) in enumerate(((0, FIRST_GATES), (FIRST_GATES, X))):
                    sp.dma_start(gates[i][:, e0:e1, :], a["scratch"][e0:e1, QB * i:QB * (i + 1)].unsqueeze(0)
                                 .broadcast_to([P, e1 - e0, QB])).then_inc(g_in[2 * i + part], 16)
            for i in range(NB):
                sp.wait_ge(y_done, i + 1)
                sp.dma_start(out[QB * i:QB * (i + 1), :].rearrange("(t p) e -> p t e", p=P),
                             x1[:, BT * i:BT * (i + 1), :]).then_inc(stored, 16)
            sp.wait_ge(stored, 16 * NB)

        @block.gpsimd
        def _(pool):
            pool.memset(vh[:], 0.0).then_inc(ones_set, 1)
            pool.wait_ge(ones_set, 1)
            pool.memset(vh[:, :, :, D:D + 1], 1.0).then_inc(ones_set, 1)
            pool.sem_inc(o_ready, 1)
            pool.wait_ge(in_c, n_consts)
            pool.wait_ge(tables, 1)
            pool.wait_ge(v_ready, NB)

            def build(it, k):
                hd = head(it, k)
                done = [0]

                def link(ins):
                    done[0] += 1
                    ins.then_inc(pool_chain, 1)
                    pool.wait_ge(pool_chain, count(it, POOL_LINKS, POOL_LINKS * k + done[0]))

                if it is not None or k >= 1:
                    pool.wait_ge(base_made, count(it, 1, k))
                apart(pool)
                pool.tensor_copy(wst[:], wqk[:, bass.ds(hd, 1), :]).then_inc(wst_ready, 1)
                pool.wait_ge(base_ready, count(it, 1, k + 1))
                link(pool.tensor_copy(mixh[:], mixt[:, bass.ds(hd, 1), :]))
                if it is not None or k >= 1:
                    pool.wait_ge(parts_ready, count(it, V, V * k))
                apart(pool)
                pool.tensor_scalar(xs[:, V - 1, :], base[:], cols[:, 2:3], None, ALU.mult).then_inc(xs_ready, 1)
                link(pool.tensor_scalar(base[:], base[:], mixh[:, 0:1], None, ALU.mult))
                for v in range(LV):
                    pool.wait_ge(fac_ready, count(it, LV, LV * k + v + 1))
                    pool.tensor_tensor(xs[:, v, :], xs[:, v, :], base[:], ALU.mult).then_inc(xs_ready, 1)
                for n, v in enumerate(BUILD_ORDER):
                    pool.wait_ge(high_ready, count(it, V, V * k + n + 1))
                    pool.tensor_tensor(xs[:, v], xs[:, v], parts[:, 0, v], ALU.subtract).then_inc(rest_ready, 1)
                for n, v in enumerate(BUILD_ORDER):
                    pool.wait_ge(middle_ready, count(it, V, V * k + n + 1))
                    pool.tensor_tensor(parts[:, 2, v], xs[:, v], parts[:, 1, v], ALU.subtract)\
                        .then_inc(parts_ready, 1)
                pool.wait_ge(maske_ready, count(it, 1, k + 1))
                for n in range(N):
                    apart(pool)
                    link(pool.tensor_scalar(maske[:, n, :], maske[:, n, :], mixh[:, n + 1:n + 2], None, ALU.mult))
                if it is not None or k >= U:
                    pool.wait_ge(pv_used, count(it, UNITS, UNITS * (k - U + 1) + PSLOTS))
                pool.tensor_tensor(masks[:, k % U, :], maske[:, 0, :], maske[:, 1, :], ALU.add).then_inc(mask_ready, 1)
                pool.tensor_copy(vh[:, k % U, :, 0:D], x1[:, :, bass.ds(hd * D, D)]).then_inc(mask_ready, 1)

            for h in range(U):
                build(None, h)

            def output(it, k):
                hd = head(it, k)
                pool.wait_ge(rz_ready, count(it, 1, k + 1))
                pool.tensor_tensor(
                    xn[:, :, bass.ds(hd * D, D)], ou[:, :, 0:D],
                    widen(rz[:], D), ALU.mult).then_inc(o_ready, 1)

            def turn(it, heads):
                for k in heads:
                    if builds(it, k):
                        build(it, k + U)
                    output(it, k)
                    if it is None and k == H - 2:
                        pool.wait_ge(x1_in, 16)
                        pool.tensor_tensor(x1, x1, bvo[:, 1:2, :].broadcast_to([P, T, E]), ALU.add)\
                            .then_inc(x1_biased, 1)
            turns(pool, turn)

        @block.scalar
        def _(act):
            act.sem_inc(exp_done, BSLOTS)
            act.sem_inc(pv_out, 1)
            act.wait_ge(small, 2)
            act.activation(dec[:], dec[:], ACT.Ln).then_inc(small_act, 1)
            act.wait_ge(small, 4)
            act.activation(mixw[:], mixw[:], ACT.Exp).then_inc(small_act, 1)
            act.wait_ge(bn_done, 2 * T)
            act.activation(rstd[:], mv[:, :, 1], ACT.Sqrt, bias=cols[:, 4:5]).then_inc(sqrt_done, 1)
            for g in range(NB):
                act.wait_ge(transposed, g + 1)
                act.activation(xT[:, QB * g:QB * (g + 1)], (MISC, PV)[g % 2][:, :], ACT.Copy).then_inc(xT_ready, 1)
            act.wait_ge(tables, 1)

            def build(it, k):
                hd = head(it, k)
                act.wait_ge(base_made, count(it, 1, k + 1))
                if it is not None or k >= 1:
                    act.wait_ge(xs_ready, count(it, V, V * k))
                act.activation(base[:], MISC[:, :], ACT.Identity, bias=bqk[:, bass.ds(hd, 1)],
                               scale=cols[:, 0:1]).then_inc(base_ready, 1)

            def factor(it, k, v):
                if v == 0 and (it is not None or k >= 1):
                    act.wait_ge(parts_ready, count(it, V, V * k))
                act.activation(xs[:, v, :], dist[:, QB * v:QB * (v + 1)], ACT.Exp,
                               scale=dec[:, bass.ds(head(it, k), 1)]).then_inc(fac_ready, 1)

            def high(it, k, v):
                act.wait_ge(xs_ready, count(it, V, V * k + v + 1))
                if v == 0 and (it is not None or k >= 1):
                    act.wait_ge(staged[(k - 1) % U], gathered(it, k - 1))
                act.activation(parts[:, 0, BUILD_ORDER[v], :], xs[:, BUILD_ORDER[v], :], ACT.Copy).then_inc(high_ready, 1)

            def middle(it, k, v):
                act.wait_ge(rest_ready, count(it, V, V * k + v + 1))
                act.activation(parts[:, 1, BUILD_ORDER[v], :], xs[:, BUILD_ORDER[v], :], ACT.Copy)\
                    .then_inc(middle_ready, 1)

            def powers(it, k):
                if it is not None or k >= 1:
                    act.wait_ge(mask_ready, count(it, 2, 2 * k))
                act.activation(maske[:, 0, :], absd[:], ACT.Exp, scale=dec[:, bass.ds(head(it, k) * 2 + H, 1)])
                act.activation(maske[:, 1, :], absd[:], ACT.Exp,
                               scale=dec[:, bass.ds(head(it, k) * 2 + (H + 1), 1)]).then_inc(maske_ready, 1)

            for h in range(U):
                build(None, h)
                for v in range(LV):
                    factor(None, h, v)
                for v in range(V):
                    high(None, h, v)
                for v in range(V):
                    middle(None, h, v)
                powers(None, h)

            def turn(it, heads):
                units = [(k, n) for k in heads for n in range(UNITS)]
                for u in range(0, len(units), GROUP):
                    units[u], units[u + 1] = units[u + 1], units[u]
                for u, (k, n) in enumerate(units):
                    i, r = divmod(n, T)
                    if r % GROUP == 0:
                        act.wait_ge(b_diag, count(it, T, T * k + diagonals(n) + 1))
                    else:
                        act.wait_ge(b_plain, count(it, UNITS - T, (UNITS - T) * k + n - diagonals(n) + 1))
                    if r == LAG + 1 and u > T:
                        evacuate(it, *((k, i - 1) if i else (k - 1, NB - 1)))
                    act.wait_ge(pv_used, count(it, UNITS, k * UNITS + n + 1))
                    act.activation(probs[:, (k * UNITS + n) % PSLOTS, :], SB[(k * UNITS + n) % BSLOTS][:, :],
                                   ACT.Exp).then_inc(exp_done, 1)
                    if builds(it, k):
                        for task, when in BUILD_TICKS:
                            if n in when:
                                tasks = {"base": build, "factor": factor, "high": high, "middle": middle,
                                         "powers": powers}
                                which = (when.index(n),) if len(when) > 1 else ()
                                tasks[task](it, k + U, *which)
                evacuate(it, heads[-1], NB - 1)

            def evacuate(it, k, i):
                act.wait_ge(pv_used, count(it, UNITS, k * UNITS + T * (i + 1) + PSLOTS))
                act.wait_ge(pvs_free, count(it, NB, k * NB + i + 1))
                act.activation(pvs[:, i % 2, :], PV[:, :], ACT.Copy).then_inc(pv_out, 1)

            turns(act, turn)

            for g in range(NB):
                act.wait_ge(oT_made, g + 1)
                act.activation(xT[:, QB * g:QB * (g + 1)], SA[g % 2][:, :], ACT.Copy).then_inc(oT_ready, 1)
            act.wait_ge(bn_done, 4 * T)
            act.activation(rstd[:], mv[:, :, 1], ACT.Sqrt, bias=cols[:, 4:5]).then_inc(sqrt_done, 1)
            for g in range(NB):
                act.wait_ge(transposed, NB + g + 1)
                act.activation(xT[:, QB * g:QB * (g + 1)], SA[g % 2][:, :], ACT.Copy).then_inc(xT_ready, 1)
            act.wait_ge(rt_step, 2)
            act.activation(lg[:], lg[:], ACT.Exp).then_inc(rt_act, 1)
            for g in range(NB):
                act.wait_ge(gT_made, g + 1)
                act.activation(gateT[0:X, QB * g:QB * (g + 1)], SB[g % 2][0:X, :], ACT.Copy).then_inc(gT_ready, 1)
            for i in range(NB):
                for u in range(X * FC):
                    g = i * X * FC + u
                    act.wait_ge(up_scaled, g + 1)
                    if g >= 4:
                        act.wait_ge(h_free, g - 3)
                    act.activation(hT[g % 4], up[g % 3], ACT.Relu).then_inc(h_ready, 1)
                act.wait_ge(h_free, X * FC * (i + 1))
                act.activation(yT[:, i, :], (PV, MISC)[i % 2][:, :], ACT.Copy).then_inc(y_out, 1)

        @block.tensor
        def _(pe):
            pe.sem_inc(pv_used, PSLOTS)
            pe.sem_inc(pvs_free, 2)
            pe.wait_ge(in_c, n_consts)
            for g in range(NB):
                pe.wait_ge(normed, BT * (g + 1))
                if g >= 2:
                    pe.wait_ge(xT_ready, g - 1)
                for t in range(BT):
                    mm = pe.transpose((MISC, PV)[g % 2][:, P * t:P * (t + 1)], xn[:, BT * g + t, :], ident[:])
                mm.then_inc(transposed, 1)
            for g in range(NB):
                pe.wait_ge(xT_ready, g + 1)
                for t in range(BT):
                    c = BT * g + t
                    mm = pe.matmul((SA[0], SA[1], SA[2], SB[0])[g][:, P * t:P * (t + 1)], xT[:, P * c:P * (c + 1)],
                                   wv[:], start=True, stop=True, skip_group_check=True)
                mm.then_inc(v_made, 1)

            def base_product(it, k):
                pe.wait_ge(wst_ready, count(it, 1, k + 1))
                for i in range(NB):
                    mm = pe.matmul(MISC[32 * i:32 * (i + 1), :], wst[:], xT[:, QB * i:QB * (i + 1)],
                                   start=True, stop=True, skip_group_check=True)
                mm.then_inc(base_made, 1)

            pe.wait_ge(xT_ready, NB)
            base_product(None, 0)

            def rows(s, used, side, v, token, n):
                c0 = token % QB
                return stage[s][0:used, side, token // QB, v, c0:c0 + n]

            def a_unit(it, k, n):
                i, b = divmod(n, NB)
                s = k % U
                g = (k * UNITS + n)
                pe.wait_ge(a_free, count(it, UNITS, g + 1))
                bank = SA[g % ASLOTS]
                for v, c0, cn in block_pieces(i // BT, b, i):
                    mm = pe.matmul(bank[:, c0:c0 + cn], rows(s, KR, 0, v, P * i, P),
                                   rows(s, KR, 1, v, QB * b + c0, cn),
                                   start=True, stop=True, skip_group_check=True)
                mm.then_inc(a_made, 1)

            def maxima(it, k):
                pe.wait_ge(nm_step, count(it, 5, 5 * (k + 1)))
                apart(pe)
                pe.transpose(MISC[:, :].bitcast(BF16)[0:3 * T, 0:P], nmp[:].rearrange("p b a t -> p (b a t)"), identb[:])\
                  .then_inc(nmT_made, 1)

            pe.wait_ge(in_rest, 16 * 2 * U)
            pe.wait_ge(base_ready, 1)
            base_product(None, 1)
            pe.wait_ge(staged[0], gathered(None, 0))
            for n in range(UNITS):
                a_unit(None, 0, n)
                if n == UNITS // 2:
                    pe.wait_ge(base_ready, 2)
                    base_product(None, 2)
            pe.wait_ge(base_ready, U)
            maxima(None, 0)
            pe.wait_ge(staged[1], gathered(None, 1))
            for n in range(AHEAD):
                a_unit(None, 1, n)

            def turn(it, heads):
                for what, k, n in timeline(it, heads):
                    i, r = divmod(n, T)
                    s = k % U
                    if what == "b":
                        if n == 0:
                            pe.wait_ge(shifted[s], shifts(it, k))
                        j = key_order(i)[r]
                        g = k * UNITS + n
                        pe.wait_ge(exp_done, count(it, UNITS, g + (2 if (g - BSLOTS) % GROUP == 0 else 1)))
                        bank = SB[g % BSLOTS]
                        for v, c0, cn in block_pieces(j // BT, i, j):
                            used = KR if v == V - 1 else P
                            mm = pe.matmul(bank[:, c0:c0 + cn], rows(s, used, 1, v, P * j, P),
                                           rows(s, used, 0, v, QB * i + c0, cn),
                                           start=True, stop=True, skip_group_check=True)
                        mm.then_inc(b_raw if j // BT == i else b_plain, 1)
                    elif what == "shift":
                        j = key_order(i)[r]
                        if j // BT != i:
                            continue
                        pe.wait_ge(b_masked, count(it, T, k * T + diagonals(n) + 1))
                        c0 = P * (j % BT)
                        pe.matmul(SB[(k * UNITS + n) % BSLOTS][:, c0:c0 + P], stage[s][KR:SH, 1, 0, 0, 0:P],
                                  stage[s][KR:SH, 0, i, 0, c0:c0 + P], start=False, stop=True,
                                  skip_group_check=True).then_inc(b_diag, 1)
                    elif what == "a":
                        m = n + AHEAD
                        if m == UNITS:
                            pe.wait_ge(staged[(k + 2) % U], gathered(it, k + 2))
                        a_unit(it, k + 1 + m // UNITS, m % UNITS)
                    elif what == "maxima":
                        pe.wait_ge(ou_step, count(it, NB, NB * k + MAXIMA_SUMS + 1))
                        maxima(it, k + 1)
                    elif what == "base":
                        pe.wait_ge(ou_step, count(it, NB, NB * k + 1))
                        pe.wait_ge(nmT_ready, count(it, 1, k + 1))
                        base_product(it, k + U)
                    elif what == "pv":
                        i, r = divmod(GROUP * n, T)
                        if n == 0:
                            pe.wait_ge(mask_ready, count(it, 2, 2 * (k + 1)))
                        if r == 0:
                            pe.wait_ge(pv_out, count(it, NB, k * NB + i + 1))
                        pe.wait_ge(exp_done, count(it, UNITS, k * UNITS + GROUP * (n + 1) + BSLOTS))
                        for c in range(GROUP):
                            pe.matmul(PV[32 * c:32 * (c + 1), :], vh[:, s, key_order(i)[r + c], :],
                                      probs[:, (k * UNITS + GROUP * n + c) % PSLOTS, :],
                                      start=(r == 0), stop=(r == T - GROUP), skip_group_check=True)\
                                .then_inc(pv_used, 1)
                    elif what == "sum":
                        i, t = divmod(n, BT)
                        if t == 0:
                            pe.wait_ge(pv_out, count(it, NB, k * NB + i + 2))
                            pe.wait_ge(ou_step, count(it, NB, NB * k + i + 1))
                            if i == 0 and builds(it, k):
                                pe.wait_ge(base_ready, count(it, 1, k + U + 1))
                            if i == MAXIMA_SUMS and (it is not None or k + 1 < H):
                                pe.wait_ge(nmT_ready, count(it, 1, k + 2))
                        mm = pe.matmul(MISC[:, (D + 1) * t:(D + 1) * (t + 1)], pvs[:, i % 2, P * t:P * (t + 1)],
                                       groups[:], start=True, stop=True, skip_group_check=True)
                        if t == BT - 1:
                            mm.then_inc(pvs_free, 1)
            turns(pe, turn)

            pe.wait_ge(o_ready, H + 1)
            for g in range(NB):
                if g >= 2:
                    pe.wait_ge(oT_ready, g - 1)
                for t in range(BT):
                    mm = pe.transpose(SA[g % 2][:, P * t:P * (t + 1)], xn[:, BT * g + t, :], ident[:])
                mm.then_inc(oT_made, 1)
            for g in range(NB):
                pe.wait_ge(oT_ready, g + 1)
                if g >= 2:
                    pe.wait_ge(x1_ready, g - 1)
                for t in range(BT):
                    c = BT * g + t
                    mm = pe.matmul(SB[g % 2][:, P * t:P * (t + 1)], xT[:, P * c:P * (c + 1)], wo[:],
                                   start=True, stop=True, skip_group_check=True)
                mm.then_inc(wo_made, 1)
            for g in range(NB):
                pe.wait_ge(normed, T + BT * (g + 1))
                if g >= 2:
                    pe.wait_ge(xT_ready, NB + g - 1)
                for t in range(BT):
                    mm = pe.transpose(SA[g % 2][:, P * t:P * (t + 1)], xn[:, BT * g + t, :], ident[:])
                mm.then_inc(transposed, 1)
            pe.wait_ge(xT_ready, 2 * NB)
            pe.wait_ge(small_in, 16 * 5)
            for t in range(T):
                mm = pe.matmul(SA[2][:, X * t:X * (t + 1)], xT[:, P * t:P * (t + 1)], wrv,
                               start=True, stop=True, skip_group_check=True)
            mm.then_inc(rt_made, 1)
            pe.wait_ge(rt_step, RT_STEPS)
            for g in range(NB):
                if g >= 2:
                    pe.wait_ge(gT_ready, g - 1)
                for t in range(BT):
                    mm = pe.transpose(SB[g % 2][0:X, P * t:P * (t + 1)], gate[:, BT * g + t, :], ident[:])
                mm.then_inc(gT_made, 1)
            pe.wait_ge(w1_in, 16)
            pe.wait_ge(w2_in, 16)
            total = NB * X * FC

            def up_product(g):
                i, u = divmod(g, X * FC)
                e, c = divmod(u, FC)
                if g >= 3:
                    pe.wait_ge(up_scaled, g - 2)
                pe.matmul(SA[g % 3][:, :], w1[:, e, P * c:P * (c + 1)], xT[:, QB * i:QB * (i + 1)],
                          start=True, stop=True, skip_group_check=True).then_inc(up_made, 1)

            def down_product(g):
                i, u = divmod(g, X * FC)
                e, c = divmod(u, FC)
                bank = (PV, MISC)[i % 2]
                if u == 0:
                    if i >= 2:
                        pe.wait_ge(y_out, i - 1)
                    pe.wait_ge(gT_ready, NB)
                    pe.matmul(bank[:, :], b2v, gateT[0:X, QB * i:QB * (i + 1)], start=True, stop=False,
                              skip_group_check=True)
                pe.wait_ge(h_ready, g + 1)
                mm = pe.matmul(bank[:, :], w2[:, e, c, :], hT[g % 4], start=False, stop=(u == X * FC - 1),
                               skip_group_check=True)
                mm.then_inc(h_free, 1)

            def y_transposes(i):
                pe.wait_ge(y_out, i + 1)
                if i >= 2:
                    pe.wait_ge(y_done, i - 1)
                for t in range(BT):
                    mm = pe.transpose(SB[i % 2][:, P * t:P * (t + 1)], yT[:, i, P * t:P * (t + 1)], ident[:])
                mm.then_inc(yT_made, 1)

            for g in range(total + 2):
                if g < total:
                    up_product(g)
                if g >= 2:
                    down_product(g - 2)
                    if (g - 2) % (X * FC) == 4 and g > X * FC:
                        y_transposes((g - 2) // (X * FC) - 1)
            y_transposes(NB - 1)

        @block.vector
        def _(dve):
            dve.sem_inc(a_free, ASLOTS)
            dve.sem_inc(ou_step, 1)

            def step_of(s, count, ins):
                count[0] += 1
                ins.then_inc(s, 1)
                dve.wait_ge(s, count[0])

            for g in range(NB):
                dve.wait_ge(in_x[g], 16)
                for t in range(BT * g, BT * (g + 1)):
                    dve.bn_stats(stats[:, t, :], x[:, t, :]).then_inc(bn_done, 1)

            dve.wait_ge(in_t, 16 * 4)
            sm = [0]
            step_of(small, sm, dve.tensor_scalar(dec[:], dec[:], 0.01, 0.9999, ALU.max, ALU.min))
            step_of(small, sm, dve.tensor_tensor(mixs[:, 0, :], mixw[:, :, 0], mixw[:, :, 1], ALU.max))
            for n in range(N):
                step_of(small, sm, dve.tensor_tensor(mixw[:, :, n], mixw[:, :, n], mixs[:, 0, :], ALU.subtract))
            dve.wait_ge(small_act, 2)
            step_of(small, sm, dve.tensor_tensor(mixs[:, 0, :], mixw[:, :, 0], mixw[:, :, 1], ALU.add))
            step_of(small, sm, dve.reciprocal(mixs[:, 1, :], mixs[:, 0, :]))
            for n in range(N):
                step_of(small, sm, dve.tensor_tensor(mixt[:, :, 1 + n], mixw[:, :, n], mixs[:, 1, :], ALU.mult))
            step_of(small, sm, dve.tensor_scalar(mixs[:, 2, :], mixt[:, :, 1], cols[:, 5:6], cols[:, 1:2],
                                                 ALU.mult, ALU.add))
            step_of(small, sm, dve.scalar_tensor_tensor(mixt[:, :, 0], mixt[:, :, 2], cols[:, 6:7], mixs[:, 2, :],
                                                        ALU.mult, ALU.add))
            step_of(small, sm, dve.tensor_scalar(bqk[:], bqk[:], cols[:, 0:1], None, ALU.mult))
            dve.sem_inc(tables, 1)

            def statistics(src, g):
                for t in range(BT * g, BT * (g + 1)):
                    dve.bn_stats(stats[:, t, :], src[:, t, :]).then_inc(bn_done, 1)

            def normalise(src, part):
                dve.wait_ge(bn_done, 2 * T * part + T)
                for t in range(T):
                    dve.bn_aggr(mv[:, t, :], stats[:, t, :]).then_inc(bn_done, 1)
                dve.wait_ge(sqrt_done, part + 1)
                dve.reciprocal(rstd[:], rstd[:]).then_inc(rstd_ready, 1)
                dve.wait_ge(rstd_ready, part + 1)
                for t in range(T):
                    dve.tensor_scalar(xn[:, t, :], src[:, t, :], mv[:, t, 0:1], rstd[:, t:t + 1],
                                      ALU.subtract, ALU.mult).then_inc(normed, 1)

            normalise(x, 0)
            dve.wait_ge(in_c, n_consts)
            dve.tensor_copy(identb[:], ident[:])
            for g in range(NB):
                dve.wait_ge(v_made, g + 1)
                bank = (SA[0], SA[1], SA[2], SB[0])[g]
                for t in range(BT):
                    ins = dve.tensor_tensor(vals[:, BT * g + t, :, :].rearrange("p h d -> p (h d)"),
                                            bank[:, P * t:P * (t + 1)], bvo[:, 0, :], ALU.add)
                ins.then_inc(v_ready, 1)

            def a_max(it, k, n):
                i, b = divmod(n, NB)
                g = k * UNITS + n
                bank = SA[g % ASLOTS]
                dve.wait_ge(a_made, count(it, UNITS, g + 1))
                if b == i // BT:
                    if n == 0:
                        dve.wait_ge(mask_ready, count(it, 2, 2 * (k + 1)))
                    tile = bank[:, P * (i % BT):P * (i % BT + 1)]
                    dve.tensor_tensor(tile, tile, masks[:, k % U, :], ALU.mult).then_inc(a_masked, 1)
                    dve.wait_ge(a_masked, count(it, T, k * T + i + 1))
                dve.tensor_reduce(mx[:, n:n + 1], bank[:, :], AX.X, ALU.max).then_inc(a_free, 1)

            def finish(it, k):
                c = [0]

                def link(ins):
                    c[0] += 1
                    ins.then_inc(nm_step, 1)
                    dve.wait_ge(nm_step, count(it, 5, 5 * k + c[0]))
                dve.wait_ge(a_free, count(it, UNITS, (k + 1) * UNITS + ASLOTS))
                link(dve.tensor_reduce(nm[:, 0, :], mx[:].rearrange("p (t b) -> p t b", b=NB), AX.X, ALU.max,
                                       negate=True))
                whole, rest = (nm[:, x, :].rearrange("p (b t) -> p b t", t=BT) for x in range(2))
                link(dve.tensor_copy(nmp[:, :, 0, :], whole))
                link(dve.tensor_tensor(rest, whole, nmp[:, :, 0, :], ALU.subtract))
                link(dve.tensor_copy(nmp[:, :, 1, :], rest))
                link(dve.tensor_tensor(nmp[:, :, 2, :], rest, nmp[:, :, 1, :], ALU.subtract))

            def maxima_out(it, k):
                dve.wait_ge(nmT_made, count(it, 1, k + 1))
                if it is not None or k >= 1:
                    dve.wait_ge(shifted[(k - 1) % U], shifts(it, k - 1))
                dve.tensor_copy(nmT[:], MISC[:, :].bitcast(BF16)[0:3 * T, 0:P]).then_inc(nmT_ready, 1)

            def first_maxima():
                for n in range(UNITS):
                    a_max(None, 0, n)
                finish(None, 0)
                maxima_out(None, 0)
                for n in range(AHEAD):
                    a_max(None, 1, n)

            first_maxima()

            def mask(it, k, n):
                i, r = divmod(n, T)
                j = key_order(i)[r]
                if j // BT != i:
                    return
                c0 = P * (j % BT)
                tile = SB[(k * UNITS + n) % BSLOTS][:, c0:c0 + P]
                dve.wait_ge(b_raw, count(it, T, k * T + diagonals(n) + 1))
                dve.tensor_tensor(tile, tile, masks[:, k % U, :], ALU.mult).then_inc(b_masked, 1)

            def turn(it, heads):
                units = [(k, n) for k in heads for n in range(UNITS)]
                order = timeline(it, heads)
                for u in range(EARLY):
                    mask(it, *units[u])
                for what, k, n in order:
                    if what == "b":
                        u = (k - heads[0]) * UNITS + n + EARLY
                        if u < len(units):
                            mask(it, *units[u])
                    elif what == "a":
                        m = n + AHEAD
                        a_max(it, k + 1 + m // UNITS, m % UNITS)
                        if m == UNITS - 1:
                            finish(it, k + 1)
                    elif what == "maxima":
                        maxima_out(it, k + 1)
                    elif what == "sum" and n % BT == BT - 1:
                        i = n // BT
                        dve.wait_ge(pvs_free, count(it, NB, k * NB + i + 3))
                        if i == 0:
                            dve.wait_ge(o_ready, count(it, 1, k + 1))
                        dve.tensor_copy(ou[:, BT * i:BT * (i + 1), :],
                                        MISC[:, 0:BT * (D + 1)].rearrange("p (t d) -> p t d", t=BT))\
                            .then_inc(ou_step, 1)
                        if i == NB - 1:
                            dve.wait_ge(ou_step, count(it, NB, NB * (k + 1) + 1))
                            dve.reciprocal(rz[:], ou[:, :, D]).then_inc(rz_ready, 1)
            turns(dve, turn)

            dve.wait_ge(x1_biased, 1)
            for g in range(NB):
                dve.wait_ge(wo_made, g + 1)
                rows = x1[:, BT * g:BT * (g + 1), :]
                dve.tensor_tensor(rows, rows, SB[g % 2][:, :].rearrange("p (t e) -> p t e", e=E), ALU.add)\
                   .then_inc(x1_ready, 1)
                dve.wait_ge(x1_ready, g + 1)
                statistics(x1, g)
            normalise(x1, 1)

            c = [0]

            def link(ins):
                step_of(rt_step, c, ins)

            dve.wait_ge(rt_made, 1)
            dve.wait_ge(small_in, 16 * 5)
            dve.tensor_tensor(lg[:], SA[2][:, 0:T * X].rearrange("p (t x) -> p t x", x=X),
                              brv.unsqueeze(1).broadcast_to([P, T, X]), ALU.add).then_inc(lg_ready, 1)
            dve.wait_ge(lg_ready, 1)
            link(dve.tensor_reduce(rt1, lg[:], AX.X, ALU.max))
            link(dve.tensor_tensor(lg[:], lg[:], widen(rt1, X), ALU.subtract))
            dve.wait_ge(rt_act, 1)
            link(dve.tensor_reduce(rt1, lg[:], AX.X, ALU.add))
            link(dve.reciprocal(rt2, rt1))
            link(dve.tensor_tensor(lg[:], lg[:], widen(rt2, X), ALU.mult))
            mine = lg.unsqueeze(3).broadcast_to([P, T, X, X])
            theirs = lg.unsqueeze(2).broadcast_to([P, T, X, X])
            tie = tiev.unsqueeze(1).broadcast_to([P, T, X, X])
            link(dve.tensor_tensor(big1, theirs, mine, ALU.is_equal))
            link(dve.tensor_tensor(big1, big1, tie, ALU.mult))
            link(dve.tensor_tensor(big2, theirs, mine, ALU.is_gt))
            link(dve.tensor_tensor(big1, big1, big2, ALU.add))
            link(dve.tensor_tensor(big1, big1, theirs, ALU.mult))
            link(dve.tensor_reduce(cum, big1, AX.X, ALU.add))
            link(dve.tensor_scalar(eq0, cum, 0.0, None, ALU.is_equal))
            link(dve.tensor_tensor(cum, cum, lg[:], ALU.add))
            link(dve.tensor_scalar(cum, cum, TOP_P, None, ALU.is_lt))
            link(dve.tensor_tensor(cum, cum, eq0, ALU.max))
            link(dve.tensor_tensor(gate, cum, lg[:], ALU.mult))

            def add_y(i):
                dve.wait_ge(yT_made, i + 1)
                rows = x1[:, BT * i:BT * (i + 1), :]
                dve.tensor_tensor(rows, rows, SB[i % 2][:, :].rearrange("p (t e) -> p t e", e=E), ALU.add)\
                   .then_inc(y_done, 1)

            for i in range(NB):
                for u in range(X * FC):
                    if u == 0:
                        dve.wait_ge(g_in[2 * i], 16)
                    if u == FIRST_GATES * FC:
                        dve.wait_ge(g_in[2 * i + 1], 16)
                    g = i * X * FC + u
                    e, c2 = divmod(u, FC)
                    dve.wait_ge(up_made, g + 1)
                    if g >= 3:
                        dve.wait_ge(h_ready, g - 2)
                    dve.scalar_tensor_tensor(up[g % 3], SA[g % 3][:, :], b1v[:, e, c2:c2 + 1], gates[i][:, e, :],
                                             ALU.add, ALU.mult).then_inc(up_scaled, 1)
                    if i >= 1 and u == 8:
                        add_y(i - 1)
            add_y(NB - 1)



FIRST_GATES = 2
RT_STEPS = 16


def kernel(**inputs):
    import concourse.bacc as _bacc
    from concourse.bass_utils import run_bass_kernel_spmd as _run

    g = {k.split("_", 1)[1]: np.asarray(v) for k, v in inputs.items()}

    def everywhere(v):
        return np.broadcast_to(v, (P,) + v.shape)

    def qk_rows(q, k):
        q, k = (np.repeat(m.reshape(H, 1, D, -1), N, 1) for m in (q, k))
        return np.stack([q, k], 1).reshape(H, 2 * ROWS, -1)

    wqk = qk_rows(g["attn_Wq"], g["attn_Wk"]).transpose(2, 0, 1)
    bqk = np.tile(qk_rows(g["attn_bq"], g["attn_bk"])[:, :, 0].T, (NB, 1))
    dec = g["attn_decay_params"]
    by_row = np.tile(np.repeat(dec.T, D, 0), (2 * NB, 1))
    token = np.arange(S).reshape(NB, 1, QB)
    dist = np.stack([np.abs(token % (2 * w) - w) for w in WIDTHS], 1).reshape(NB, 1, LV * QB)
    lane = np.arange(P)
    query, second = lane // ROWS % 2 == 0, lane // D % 2 == 1
    cols = np.zeros((P, 8), np.float32)
    cols[:, 0] = np.where(query, D ** -0.5, 1)
    cols[:, 1] = ~query
    cols[:, 2] = np.where(query, 1 / N, 1)
    cols[:, 4] = EPS
    cols[:, 5] = query & ~second
    cols[:, 6] = query & second
    lower = np.arange(X)[None, :] < np.arange(X)[:, None]
    arrays = {
        "x": g["attn_x"].reshape(S, E),
        "wqk": wqk, "bqk": bqk, "wv": g["attn_Wv"].T, "wo": g["attn_Wo"].T,
        "bvo": everywhere(np.stack([g["attn_bv"], g["attn_bo"]])),
        "dec": np.concatenate([by_row, everywhere(dec.reshape(-1))], 1),
        "mix": everywhere(g["attn_mix_weights"]),
        "wr": g["ffn_Wr"], "br": everywhere(g["ffn_br"]),
        "w1": g["ffn_W1"].transpose(1, 0, 2),
        "b1": g["ffn_b1"].reshape(X, FC, P).transpose(2, 0, 1),
        "w2": g["ffn_W2"].reshape(X, FC, P, E).transpose(2, 0, 1, 3),
        "b2": g["ffn_b2"],
        "c_ident": np.eye(P, dtype=np.float32),
        "c_cols": cols,
        "c_groups": np.tile(np.eye(2 * ROWS, D + 1, dtype=np.float32), (NB, 1)),
        "c_dist": np.broadcast_to(dist, (NB, 2 * ROWS, LV * QB)).reshape(P, LV * QB).astype(np.float16),
        "c_absd": np.abs(lane[:, None] - lane[None, :]).astype(np.float32),
        "c_rest": np.repeat([1.0, 0.0], (SH - KR, P - SH)).reshape(-1, 1, 1, 1).repeat(NB, 1)
        .repeat(V, 2).repeat(QB, 3).astype(mybir.dt.np(BF16)),
        "c_tie": everywhere(lower.astype(np.float32)),
    }
    nc = _bacc.Bacc("TRN2", target_bir_lowering=False, num_devices=1)
    aps, feed = {}, {}
    for name, v in arrays.items():
        feed[f"in_{name}"] = np.ascontiguousarray(v)
        aps[name] = nc.dram_tensor(f"in_{name}", v.shape, mybir.dt.from_np(v.dtype), kind="ExternalInput").ap()
    aps["scratch"] = nc.dram_tensor("scratch", (X, S), F32, kind="Internal").ap()
    out = nc.dram_tensor("out", (S, E), F32, kind="ExternalOutput").ap()
    build_program(nc, aps, out)
    r = _run(nc, [feed], core_ids=[0])
    return r.results[0]["out"].reshape(1, S, E)
```

```python
from contextlib import ExitStack

import numpy as np

import concourse.bass as bass
from concourse import mybir

ALU = mybir.AluOpType
ACT = mybir.ActivationFunctionType
AX = mybir.AxisListType
F32 = mybir.dt.float32
BF16 = mybir.dt.bfloat16
F16 = mybir.dt.float16
F32R = mybir.dt.float32r

P = 128
S = 2048
E = 128
H, D, N = 16, 8, 2
T = S // P
QB = 512
NB = S // QB
BT = QB // P
X, F = 8, 512
FC = F // P
EPS = 1e-5
TOP_P = 0.8

WIDTHS = (1024, 512, 256, 128)
LV = len(WIDTHS)
V = LV + 1
ROWS = N * D
PAIRS = ((0, 0), (0, 1), (0, 2), (1, 0), (1, 1), (2, 0))
RUNS = ((0, 3), (3, 2), (5, 1))
KR = len(PAIRS) * ROWS
SH = KR + 3

ASLOTS, BSLOTS, PSLOTS = 3, 3, 6
U = 3
STEPS_IN_LOOP = 12
GROUP = 4
LAG = 3
EARLY = 1
AHEAD = 20
BUILD_ORDER = (V - 1,) + tuple(range(LV))
BUILD_LINKS = 2 + N
UNITS = T * NB
BASE_TICK, FACTOR_TICKS, HIGH_TICKS = 15, (17, 21, 23, 25), (27, 29, 31, 37, 39)
MIDDLE_TICKS, POWERS_TICK = (41, 43, 45, 47, 53), 59
MAXIMA_SUMS = 2


def block_pieces(own, other, tile):
    if own != other:
        v = 0 if own // 2 != other // 2 else 1
        return [(v, 0, QB)]
    a = tile % BT
    return [(2, 256 * (1 - a // 2), 256), (3, 128 * (a ^ 1), 128), (V - 1, 128 * a, 128)]


def key_order(block):
    diag = [BT * block + a for a in range(BT)]
    rest = [j for j in range(T) if j // BT != block]
    out = []
    for a in range(BT):
        out += [diag[a]] + rest[3 * a:3 * a + 3]
    return out


def diagonals(n):
    return sum(key_order(u // T)[u % T] // BT == u // T for u in range(n))


def build_program(nc, a, out):
    ctx = ExitStack()
    with ctx:
        def sb(name, shape, dt=F32):
            return ctx.enter_context(nc.sbuf_tensor(name, shape, dt))

        def sem(name):
            return ctx.enter_context(nc.semaphore(name))

        xn = sb("xn", [P, T, E])
        ident = sb("ident", [P, P])
        identb = sb("identb", [P, P], BF16)
        dist = sb("dist", [P, LV * QB], F16)
        absd = sb("absd", [P, P])
        groups = sb("groups", [P, D + 1])
        cols = sb("cols", [P, 8])
        wqk = sb("wqk", [P, H, 2 * ROWS])
        wv = sb("wv", [P, E])
        wo = sb("wo", [P, E])
        bvo = sb("bvo", [P, 2, E])
        bqk = sb("bqk", [P, H])
        dec = sb("dec", [P, H + 2 * H])
        mixw = sb("mixw", [P, H, N])
        mixs = sb("mixs", [P, 3, H])
        mixt = sb("mixt", [P, H, 1 + N])
        mixh = sb("mixh", [P, 1 + N])
        stats = sb("stats", [P, T, 6])
        mv = sb("mv", [P, T, 2])
        rstd = sb("rstd", [P, T])
        wst = sb("wst", [P, 2 * ROWS])
        masks = sb("masks", [P, U, P])
        maske = sb("maske", [P, 2, P])
        vals = sb("vals", [P, T, H, D])
        vh = sb("vh", [P, U, T, 32])
        pvs = sb("pvs", [P, 2, QB])
        mx = sb("mx", [P, T * NB])
        nm = sb("nm", [P, 2, T])
        nmp = sb("nmp", [P, NB, 3, BT], BF16)
        nmT = sb("nmT", [3 * T, P], BF16)
        ou = sb("ou", [P, T, D + 1])
        rz = sb("rz", [P, T])

        with ExitStack() as attention:
            def attn(name, shape, dt=F32):
                return attention.enter_context(nc.sbuf_tensor(name, shape, dt))

            stage = [attn(f"stage{s}", [P, 2, NB, V, QB], BF16) for s in range(U)]
            parts = attn("parts", [P, 3, V, QB], BF16)
            xs = attn("xs", [P, V, QB])
            base = attn("base", [P, QB])
            probs = attn("probs", [P, PSLOTS, QB])
            xT = attn("xT", [P, S])
        slot = 2 * NB * V * QB // 2
        sb("ffn_over_stage0", [P, slot])
        w_low = sb("w_low", [P, 2 * X * F], F32R)
        sb("ffn_over_stage1", [P, slot - 2 * X * F])
        w_high = sb("w_high_part", [P, 2 * X * F], F32R)
        sb("ffn_over_stage2", [P, slot - 2 * X * F])
        sb("up_over_parts", [P, 2 * QB])
        xL = sb("xL", [P, S], F32R)
        sb("ffn_over_parts", [P, 3 * V * QB // 2 - 2 * QB - S])
        hidden = sb("hidden", [P, 2, 4, QB], F32R)
        sb("ffn_over_probs", [P, PSLOTS - 2, QB])
        xH = sb("xH", [P, S], F32R)

        SA = [ctx.enter_context(nc.psum_tensor(f"SA{i}", [P, QB], F32)) for i in range(ASLOTS)]
        SB = [ctx.enter_context(nc.psum_tensor(f"SB{i}", [P, QB], F32)) for i in range(BSLOTS)]
        PV = ctx.enter_context(nc.psum_tensor("PV", [P, QB], F32))
        MISC = ctx.enter_context(nc.psum_tensor("MISC", [P, QB], F32))

        in_x = [sem(f"in_x{i}") for i in range(NB)]
        in_c = sem("in_c")
        in_t = sem("in_t")
        in_rest = sem("in_rest")
        passed = sem("passed")
        ones_set = sem("ones_set")
        bn_done = sem("bn_done")
        rstd_ready = sem("rstd_ready")
        sqrt_done = sem("sqrt_done")
        normed = sem("normed")
        transposed = sem("transposed")
        xT_ready = sem("xT_ready")
        v_made = sem("v_made")
        v_ready = sem("v_ready")
        small = sem("small")
        small_act = sem("small_act")
        tables = sem("tables")

        wst_ready = sem("wst_ready")
        base_made = sem("base_made")
        base_ready = sem("base_ready")
        fac_ready = sem("fac_ready")
        maske_ready = sem("maske_ready")
        xs_ready = sem("xs_ready")
        high_ready = sem("high_ready")
        rest_ready = sem("rest_ready")
        middle_ready = sem("middle_ready")
        build_chain = sem("build_chain")
        parts_ready = sem("parts_ready")
        mask_ready = sem("mask_ready")
        staged = [sem(f"staged{s}") for s in range(U)]
        shifted = [sem(f"shifted{s}") for s in range(U)]

        a_made = sem("a_made")
        a_free = sem("a_free")
        a_masked = sem("a_masked")
        b_plain = sem("b_plain")
        b_raw = sem("b_raw")
        b_masked = sem("b_masked")
        b_diag = sem("b_diag")
        exp_done = sem("exp_done")
        pv_used = sem("pv_used")
        pv_out = sem("pv_out")
        pvs_free = sem("pvs_free")
        ou_step = sem("ou_step")
        rz_ready = sem("rz_ready")
        o_ready = sem("o_ready")
        nm_step = sem("nm_step")
        nmT_made = sem("nmT_made")
        nmT_ready = sem("nmT_ready")

        x1_in = sem("x1_in")
        small_in = sem("small_in")
        w1_in, w2_in = sem("w1_in"), sem("w2_in")
        oT_made, oT_ready = sem("oT_made"), sem("oT_ready")
        wo_made = sem("wo_made")
        x1_biased = sem("x1_biased")
        x1_ready = sem("x1_ready")
        rt_made = sem("rt_made")
        lg_ready = sem("lg_ready")
        rt_step, rt_act = sem("rt_step"), sem("rt_act")
        gT_made, gT_ready = sem("gT_made"), sem("gT_ready")
        g_out = sem("g_out")
        g_in = [sem(f"g_in{i}") for i in range(NB * 2)]
        x2T_ready = sem("x2T_ready")
        xL_ready = sem("xL_ready")
        w_rounded, w_split = sem("w_rounded"), sem("w_split")
        up_made = sem("up_made")
        up_out = sem("up_out")
        up_scaled = sem("up_scaled")
        h_high = sem("h_high")
        h_ready = sem("h_ready")
        h_free = sem("h_free")
        y_out, yT_made = sem("y_out"), sem("yT_made")
        y_done, stored = sem("y_done"), sem("stored")

        n_consts = 8 * 16

        class Turn:
            def __init__(self, eng, index, value):
                self.eng, self.index, self.value = eng, index, value

        def count_turns(it, per_turn, n):
            if it is None:
                return n
            it.eng.reg_add(it.value, it.index * per_turn, n)
            return it.value

        def count(it, per_head, n):
            return count_turns(it, U * per_head, n)

        def apart(eng):
            eng.sem_inc(passed, 1)

        def head(it, k):
            return k if it is None else it.index * U + k

        def gathered(it, k):
            n = 16 * 2 * len(RUNS) * NB
            return count_turns(it, n, (k // U + 1) * n)

        def shifts(it, k):
            n = 16 * LV * NB
            return count_turns(it, n, (k // U + 1) * n)

        def turns(eng, body):
            value = eng.alloc_register("wait_value")
            with eng.Fori(0, STEPS_IN_LOOP // U) as index:
                body(Turn(eng, index, value), range(U))
            body(None, range(STEPS_IN_LOOP, H))

        def builds(it, k):
            return it is not None or k + U < H

        def timeline(it, heads):
            units = [(k, n) for k in heads for n in range(UNITS)]
            seq = []
            for u in range(len(units) + LAG + 9):
                if u < len(units):
                    k, n = units[u]
                    m = n + AHEAD
                    ahead = it is not None or k + 1 + m // UNITS < H
                    seq.append(("b", k, n))
                if 1 <= u <= len(units):
                    seq.append(("shift",) + units[u - 1])
                if u < len(units):
                    if ahead:
                        seq.append(("a", k, n))
                    if n == UNITS - AHEAD + 3 and (it is not None or k + 1 < H):
                        seq.append(("maxima", k, 0))
                    if n == 12 and builds(it, k):
                        seq.append(("base", k, 0))
                if u >= LAG and u - LAG < len(units) and (u - LAG) % GROUP == GROUP - 1:
                    k, n = units[u - LAG]
                    seq.append(("pv", k, n // GROUP))
                w = u - LAG - 5
                if T <= w + 1 < len(units) + BT and (w + 1) % T < BT:
                    k, n = units[(w + 1) // T * T - 1]
                    seq.append(("sum", k, n // T * BT + (w + 1) % T))
            return seq

        def widen(ap, n):
            return ap.unsqueeze(2).broadcast_to([P, T, n])

        f0 = stage[0][:].rearrange("p a b v q -> p (a b v q)").bitcast(F32)
        f1 = stage[1][:].rearrange("p a b v q -> p (a b v q)").bitcast(F32)
        f2 = stage[2][:].rearrange("p a b v q -> p (a b v q)").bitcast(F32)
        FW = X * F
        x = f2[:, 0:T * E].rearrange("p (t e) -> p t e", e=E)
        x1 = vals[:].rearrange("p t h d -> p t (h d)")

        w1 = f1[:, 0:FW].rearrange("p (x f) -> p x f", x=X)
        w2 = f1[:, FW:2 * FW].rearrange("p (x c h) -> p x c h", x=X, c=FC)
        w1h, w1l = (w[:, 0:FW].rearrange("p (x f) -> p x f", x=X) for w in (w_high, w_low))
        w2h, w2l = (w[:, FW:2 * FW].rearrange("p (x c h) -> p x c h", x=X, c=FC) for w in (w_high, w_low))
        gates = [f0[:, (i % 2) * X * QB:(i % 2 + 1) * X * QB].rearrange("p (x q) -> p x q", x=X)
                 for i in range(NB)]
        o1 = 2 * FW
        b1v = f1[:, o1:o1 + X * FC].rearrange("p (x c) -> p x c", x=X)
        wrv = f1[:, o1 + 32:o1 + 40]
        brv = f1[:, o1 + 40:o1 + 48]
        b2v = f1[0:X, o1 + 48:o1 + 48 + E]
        tiev = f1[:, o1 + 256:o1 + 320].rearrange("p (a b) -> p a b", a=X)
        lg = f1[:, o1 + 320:o1 + 448].rearrange("p (t x) -> p t x", x=X)
        gate = f1[:, o1 + 448:o1 + 576].rearrange("p (t x) -> p t x", x=X)
        rt1 = f1[:, o1 + 576:o1 + 592]
        rt2 = f1[:, o1 + 592:o1 + 608]
        cum = f1[:, o1 + 608:o1 + 736].rearrange("p (t x) -> p t x", x=X)
        eq0 = f1[:, o1 + 736:o1 + 864].rearrange("p (t x) -> p t x", x=X)
        oz = 2 * X * QB
        big1 = f0[:, oz:oz + T * X * X].rearrange("p (t a b) -> p t a b", a=X, b=X)
        big2 = f2[:, oz:oz + T * X * X].rearrange("p (t a b) -> p t a b", a=X, b=X)
        x2T = xn[:].rearrange("p t e -> p (t e)")
        gateT = xn[:].rearrange("p t e -> p (t e)")
        free = parts[:].rearrange("p a v q -> p (a v q)").bitcast(F32)
        up = [free[:, 0:QB], free[:, QB:2 * QB], pvs[:, 0, :], pvs[:, 1, :]]
        hH, hL = ([hidden[:, part, i, :] for i in range(4)] for part in range(2))
        yT = probs[:, 2:2 + NB, :]

        def build_vectors(eng, it, k):
            hd = head(it, k)
            done = [0]

            def link(ins):
                done[0] += 1
                ins.then_inc(build_chain, 1)
                eng.wait_ge(build_chain, count(it, BUILD_LINKS, BUILD_LINKS * k + done[0]))

            if it is not None or k >= 1:
                eng.wait_ge(base_made, count(it, 1, k))
            apart(eng)
            eng.tensor_copy(wst[:], wqk[:, bass.ds(hd, 1), :]).then_inc(wst_ready, 1)
            eng.wait_ge(base_ready, count(it, 1, k + 1))
            link(eng.tensor_copy(mixh[:], mixt[:, bass.ds(hd, 1), :]))
            if it is not None or k >= 1:
                eng.wait_ge(parts_ready, count(it, V, V * k))
            apart(eng)
            eng.tensor_scalar(xs[:, V - 1, :], base[:], cols[:, 2:3], None, ALU.mult).then_inc(xs_ready, 1)
            link(eng.tensor_scalar(base[:], base[:], mixh[:, 0:1], None, ALU.mult))
            for v in range(LV):
                eng.wait_ge(fac_ready, count(it, LV, LV * k + v + 1))
                eng.tensor_tensor(xs[:, v, :], xs[:, v, :], base[:], ALU.mult).then_inc(xs_ready, 1)
            for n, v in enumerate(BUILD_ORDER):
                eng.wait_ge(high_ready, count(it, V, V * k + n + 1))
                eng.tensor_tensor(xs[:, v], xs[:, v], parts[:, 0, v], ALU.subtract).then_inc(rest_ready, 1)
            for n, v in enumerate(BUILD_ORDER):
                eng.wait_ge(middle_ready, count(it, V, V * k + n + 1))
                eng.tensor_tensor(parts[:, 2, v], xs[:, v], parts[:, 1, v], ALU.subtract)\
                    .then_inc(parts_ready, 1)
            eng.wait_ge(maske_ready, count(it, 1, k + 1))
            for n in range(N):
                apart(eng)
                link(eng.tensor_scalar(maske[:, n, :], maske[:, n, :], mixh[:, n + 1:n + 2], None, ALU.mult))
            if it is not None or k >= U:
                eng.wait_ge(pv_used, count(it, UNITS, UNITS * (k - U + 1) + PSLOTS))
            eng.tensor_tensor(masks[:, k % U, :], maske[:, 0, :], maske[:, 1, :], ALU.add).then_inc(mask_ready, 1)
            eng.tensor_copy(vh[:, k % U, :, 0:D], x1[:, :, bass.ds(hd * D, D)]).then_inc(mask_ready, 1)

        block = ctx.enter_context(nc.Block())

        @block.sync
        def _(sp):
            for i in range(NB):
                sp.dma_start(x[:, BT * i:BT * (i + 1), :],
                             a["x"][QB * i:QB * (i + 1), :].rearrange("(t p) e -> p t e", p=P)).then_inc(in_x[i], 16)
            for dst, name in ((cols, "c_cols"), (dec, "dec"), (mixw, "mix"), (bqk, "bqk")):
                sp.dma_start(dst[:], a[name]).then_inc(in_t, 16)
            for dst, name in ((ident, "c_ident"), (wqk, "wqk"), (wv, "wv"), (bvo, "bvo"), (dist, "c_dist"),
                              (absd, "c_absd"), (groups, "c_groups"), (wo, "wo")):
                sp.dma_start(dst[:], a[name]).then_inc(in_c, 16)
            for s in range(U):
                sp.dma_start(stage[s][KR:P, 1], a["c_rest"]).then_inc(in_rest, 16)
            for s in range(U):
                if s == U - 1:
                    sp.wait_ge(normed, T)
                sp.dma_start(stage[s][SH:P, 0], a["c_rest"][SH - KR:]).then_inc(in_rest, 16)

            def gather(it, k):
                s = k % U
                sp.wait_ge(parts_ready, count(it, V, V * (k + 1)))
                for c, n in RUNS:
                    for side in range(2):
                        for i in range(NB):
                            p0 = 2 * ROWS * i + ROWS * side
                            src = parts[p0:p0 + ROWS, 0:n, :, :] if side else \
                                parts[p0:p0 + ROWS, PAIRS[c][0]:PAIRS[c][0] + 1, :, :].broadcast_to([ROWS, n, V, QB])
                            sp.dma_start(stage[s][ROWS * c:ROWS * (c + n), side, i, :, :],
                                         src).then_inc(staged[s], 16)

            def maxima_rows(it, k):
                s = k % U
                sp.wait_ge(nmT_ready, count(it, 1, k + 1))
                apart(sp)
                for i in range(NB):
                    for v in range(LV):
                        sp.dma_start(stage[s][KR:SH, 0, i, v, :], nmT[3 * BT * i:3 * BT * (i + 1), :])\
                            .then_inc(shifted[s], 16)

            for h in range(U - 1):
                gather(None, h)
            maxima_rows(None, 0)
            gather(None, U - 1)

            def turn(it, heads):
                for k in heads:
                    if it is not None or k + 1 < H:
                        maxima_rows(it, k + 1)
                    sp.wait_ge(exp_done, count(it, UNITS, UNITS * (k + 1) + BSLOTS))
                    apart(sp)
                    if builds(it, k):
                        gather(it, k + U)
                    if it is None and k == H - U:
                        sp.wait_ge(mask_ready, 2 * H)
                        sp.dma_start(x1, a["x"].rearrange("(t p) e -> p t e", p=P)).then_inc(x1_in, 16)
                        for dst, name, s in ((wrv, "wr", small_in), (brv, "br", small_in), (b1v, "b1", small_in),
                                             (b2v, "b2", small_in), (tiev, "c_tie", small_in), (w1, "w1", w1_in),
                                             (w2, "w2", w2_in)):
                            sp.dma_start(dst, a[name]).then_inc(s, 16)
            turns(sp, turn)

            sp.wait_ge(gT_ready, 4)
            sp.dma_start(a["scratch"], gateT[0:X, :]).then_inc(g_out, 16)
            sp.wait_ge(g_out, 16)
            for i in range(NB):
                if i >= 2:
                    sp.wait_ge(up_scaled, X * FC * (i - 1))
                for part, (e0, e1) in enumerate(((0, FIRST_GATES), (FIRST_GATES, X))):
                    sp.dma_start(gates[i][:, e0:e1, :], a["scratch"][e0:e1, QB * i:QB * (i + 1)].unsqueeze(0)
                                 .broadcast_to([P, e1 - e0, QB])).then_inc(g_in[2 * i + part], 16)
            for i in range(NB):
                sp.wait_ge(y_done, i + 1)
                sp.dma_start(out[QB * i:QB * (i + 1), :].rearrange("(t p) e -> p t e", p=P),
                             x1[:, BT * i:BT * (i + 1), :]).then_inc(stored, 16)
            sp.wait_ge(stored, 16 * NB)

        @block.gpsimd
        def _(pool):
            pool.memset(vh[:], 0.0).then_inc(ones_set, 1)
            pool.wait_ge(ones_set, 1)
            pool.memset(vh[:, :, :, D:D + 1], 1.0).then_inc(ones_set, 1)
            pool.sem_inc(o_ready, 1)

            pool.wait_ge(mask_ready, 2)
            for h in range(1, U):
                build_vectors(pool, None, h)

            def output(it, k):
                hd = head(it, k)
                pool.wait_ge(rz_ready, count(it, 1, k + 1))
                pool.tensor_tensor(
                    xn[:, :, bass.ds(hd * D, D)], ou[:, :, 0:D],
                    widen(rz[:], D), ALU.mult).then_inc(o_ready, 1)

            def turn(it, heads):
                for k in heads:
                    if builds(it, k):
                        build_vectors(pool, it, k + U)
                    output(it, k)
                    if it is None and k == H - 2:
                        pool.wait_ge(x1_in, 16)
                        pool.tensor_tensor(x1, x1, bvo[:, 1:2, :].broadcast_to([P, T, E]), ALU.add)\
                            .then_inc(x1_biased, 1)
            turns(pool, turn)

            for n, (whole, high, low) in enumerate(((w1, w1h, w1l), (w2, w2h, w2l))):
                pool.wait_ge(w_rounded, n + 1)
                pool.tensor_tensor(low, whole, high.bitcast(F32), ALU.subtract).then_inc(w_split, 1)
            for g in range(NB * X * FC):
                pool.wait_ge(h_high, g + 1)
                pool.tensor_tensor(hL[g % 4], up[g % 4], hH[g % 4].bitcast(F32), ALU.subtract).then_inc(h_ready, 1)

        @block.scalar
        def _(act):
            act.sem_inc(exp_done, BSLOTS)
            act.sem_inc(pv_out, 1)
            act.wait_ge(small, 2)
            act.activation(dec[:], dec[:], ACT.Ln).then_inc(small_act, 1)
            act.wait_ge(small, 4)
            act.activation(mixw[:], mixw[:], ACT.Exp).then_inc(small_act, 1)
            act.wait_ge(bn_done, 2 * T)
            act.activation(rstd[:], mv[:, :, 1], ACT.Sqrt, bias=cols[:, 4:5]).then_inc(sqrt_done, 1)
            for g in range(NB):
                act.wait_ge(transposed, g + 1)
                act.activation(xT[:, QB * g:QB * (g + 1)], (MISC, PV)[g % 2][:, :], ACT.Copy).then_inc(xT_ready, 1)
            act.wait_ge(tables, 1)

            def build(it, k):
                hd = head(it, k)
                act.wait_ge(base_made, count(it, 1, k + 1))
                if it is not None or k >= 1:
                    act.wait_ge(xs_ready, count(it, V, V * k))
                act.activation(base[:], MISC[:, :], ACT.Identity, bias=bqk[:, bass.ds(hd, 1)],
                               scale=cols[:, 0:1]).then_inc(base_ready, 1)

            def factor(it, k, v):
                if v == 0 and (it is not None or k >= 1):
                    act.wait_ge(parts_ready, count(it, V, V * k))
                act.activation(xs[:, v, :], dist[:, QB * v:QB * (v + 1)], ACT.Exp,
                               scale=dec[:, bass.ds(head(it, k), 1)]).then_inc(fac_ready, 1)

            def high(it, k, v):
                act.wait_ge(xs_ready, count(it, V, V * k + v + 1))
                if v == 0 and (it is not None or k >= 1):
                    act.wait_ge(staged[(k - 1) % U], gathered(it, k - 1))
                act.activation(parts[:, 0, BUILD_ORDER[v], :], xs[:, BUILD_ORDER[v], :], ACT.Copy)\
                    .then_inc(high_ready, 1)

            def middle(it, k, v):
                act.wait_ge(rest_ready, count(it, V, V * k + v + 1))
                act.activation(parts[:, 1, BUILD_ORDER[v], :], xs[:, BUILD_ORDER[v], :], ACT.Copy)\
                    .then_inc(middle_ready, 1)

            def powers(it, k):
                if it is not None or k >= 1:
                    act.wait_ge(mask_ready, count(it, 2, 2 * k))
                act.activation(maske[:, 0, :], absd[:], ACT.Exp, scale=dec[:, bass.ds(head(it, k) * 2 + H, 1)])
                act.activation(maske[:, 1, :], absd[:], ACT.Exp,
                               scale=dec[:, bass.ds(head(it, k) * 2 + (H + 1), 1)]).then_inc(maske_ready, 1)

            for h in range(U):
                build(None, h)
                for v in range(LV):
                    factor(None, h, v)
                for v in range(V):
                    high(None, h, v)
                for v in range(V):
                    middle(None, h, v)
                powers(None, h)

            def turn(it, heads):
                units = [(k, n) for k in heads for n in range(UNITS)]
                for u in range(0, len(units), GROUP):
                    units[u], units[u + 1] = units[u + 1], units[u]
                for u, (k, n) in enumerate(units):
                    i, r = divmod(n, T)
                    if r % GROUP == 0:
                        act.wait_ge(b_diag, count(it, T, T * k + diagonals(n) + 1))
                    else:
                        act.wait_ge(b_plain, count(it, UNITS - T, (UNITS - T) * k + n - diagonals(n) + 1))
                    if r == LAG + 1 and u > T:
                        evacuate(it, *((k, i - 1) if i else (k - 1, NB - 1)))
                    act.wait_ge(pv_used, count(it, UNITS, k * UNITS + n + 1))
                    act.activation(probs[:, (k * UNITS + n) % PSLOTS, :], SB[(k * UNITS + n) % BSLOTS][:, :],
                                   ACT.Exp).then_inc(exp_done, 1)
                    if builds(it, k):
                        if n == BASE_TICK:
                            build(it, k + U)
                        if n in FACTOR_TICKS:
                            factor(it, k + U, FACTOR_TICKS.index(n))
                        if n in HIGH_TICKS:
                            high(it, k + U, HIGH_TICKS.index(n))
                        if n in MIDDLE_TICKS:
                            middle(it, k + U, MIDDLE_TICKS.index(n))
                        if n == POWERS_TICK:
                            powers(it, k + U)
                evacuate(it, heads[-1], NB - 1)

            def evacuate(it, k, i):
                act.wait_ge(pv_used, count(it, UNITS, k * UNITS + T * (i + 1) + PSLOTS))
                act.wait_ge(pvs_free, count(it, NB, k * NB + i + 1))
                act.activation(pvs[:, i % 2, :], PV[:, :], ACT.Copy).then_inc(pv_out, 1)

            turns(act, turn)

            for g in range(NB):
                act.wait_ge(oT_made, g + 1)
                act.activation(xT[:, QB * g:QB * (g + 1)], SA[g % 2][:, :], ACT.Copy).then_inc(oT_ready, 1)
            act.wait_ge(w1_in, 16)
            act.activation(w1h, w1, ACT.Copy).then_inc(w_rounded, 1)
            act.wait_ge(bn_done, 4 * T)
            act.activation(rstd[:], mv[:, :, 1], ACT.Sqrt, bias=cols[:, 4:5]).then_inc(sqrt_done, 1)
            for g in range(NB):
                act.wait_ge(transposed, NB + g + 1)
                block = slice(QB * g, QB * (g + 1))
                act.activation(x2T[:, block], SA[g % 2][:, :], ACT.Copy).then_inc(x2T_ready, 1)
                act.wait_ge(x2T_ready, g + 1)
                act.activation(xH[:, block], x2T[:, block], ACT.Copy).then_inc(xT_ready, 1)
            act.wait_ge(rt_step, 2)
            act.activation(lg[:], lg[:], ACT.Exp).then_inc(rt_act, 1)
            act.wait_ge(w2_in, 16)
            act.activation(w2h, w2, ACT.Copy).then_inc(w_rounded, 1)
            for g in range(NB):
                act.wait_ge(gT_made, g + 1)
                act.activation(gateT[0:X, QB * g:QB * (g + 1)], SB[g % 2][0:X, :], ACT.Copy).then_inc(gT_ready, 1)

            def high_part(g):
                act.wait_ge(up_scaled, g + 1)
                if g >= 4:
                    act.wait_ge(h_free, g - 3)
                act.activation(hH[g % 4], up[g % 4], ACT.Copy).then_inc(h_high, 1)

            def y_copy(i):
                act.wait_ge(h_free, X * FC * (i + 1))
                act.activation(yT[:, i, :], (PV, MISC)[i % 2][:, :], ACT.Copy).then_inc(y_out, 1)

            for g in range(NB * X * FC):
                i, u = divmod(g, X * FC)
                e, c = divmod(u, FC)
                act.wait_ge(up_made, g + 1)
                if g >= 4:
                    act.wait_ge(h_ready, g - 3)
                act.activation(up[g % 4], SA[g % 3][:, :], ACT.Relu, bias=b1v[:, e, c:c + 1]).then_inc(up_out, 1)
                if g >= 1:
                    high_part(g - 1)
                if i >= 1 and u == DOWN_LAG + 2:
                    y_copy(i - 1)
            high_part(NB * X * FC - 1)
            y_copy(NB - 1)

        @block.tensor
        def _(pe):
            pe.sem_inc(pv_used, PSLOTS)
            pe.sem_inc(pvs_free, 2)
            pe.wait_ge(in_c, n_consts)
            for g in range(NB):
                pe.wait_ge(normed, BT * (g + 1))
                if g >= 2:
                    pe.wait_ge(xT_ready, g - 1)
                for t in range(BT):
                    mm = pe.transpose((MISC, PV)[g % 2][:, P * t:P * (t + 1)], xn[:, BT * g + t, :], ident[:])
                mm.then_inc(transposed, 1)
            for g in range(NB):
                pe.wait_ge(xT_ready, g + 1)
                for t in range(BT):
                    c = BT * g + t
                    mm = pe.matmul((SA[0], SA[1], SA[2], SB[0])[g][:, P * t:P * (t + 1)], xT[:, P * c:P * (c + 1)],
                                   wv[:], start=True, stop=True, skip_group_check=True)
                mm.then_inc(v_made, 1)

            def base_product(it, k):
                pe.wait_ge(wst_ready, count(it, 1, k + 1))
                for i in range(NB):
                    mm = pe.matmul(MISC[32 * i:32 * (i + 1), :], wst[:], xT[:, QB * i:QB * (i + 1)],
                                   start=True, stop=True, skip_group_check=True)
                mm.then_inc(base_made, 1)

            pe.wait_ge(xT_ready, NB)
            base_product(None, 0)

            def rows(s, used, side, v, token, n):
                c0 = token % QB
                return stage[s][0:used, side, token // QB, v, c0:c0 + n]

            def a_unit(it, k, n):
                i, b = divmod(n, NB)
                s = k % U
                g = (k * UNITS + n)
                pe.wait_ge(a_free, count(it, UNITS, g + 1))
                bank = SA[g % ASLOTS]
                for v, c0, cn in block_pieces(i // BT, b, i):
                    mm = pe.matmul(bank[:, c0:c0 + cn], rows(s, KR, 0, v, P * i, P),
                                   rows(s, KR, 1, v, QB * b + c0, cn),
                                   start=True, stop=True, skip_group_check=True)
                mm.then_inc(a_made, 1)

            def maxima(it, k):
                pe.wait_ge(nm_step, count(it, 5, 5 * (k + 1)))
                apart(pe)
                pe.transpose(MISC[:, :].bitcast(BF16)[0:3 * T, 0:P], nmp[:].rearrange("p b a t -> p (b a t)"), identb[:])\
                  .then_inc(nmT_made, 1)

            pe.wait_ge(in_rest, 16 * 2 * U)
            pe.wait_ge(base_ready, 1)
            base_product(None, 1)
            pe.wait_ge(staged[0], gathered(None, 0))
            for n in range(UNITS):
                a_unit(None, 0, n)
                if n == UNITS // 2:
                    pe.wait_ge(base_ready, 2)
                    base_product(None, 2)
            pe.wait_ge(base_ready, U)
            maxima(None, 0)
            pe.wait_ge(staged[1], gathered(None, 1))
            for n in range(AHEAD):
                a_unit(None, 1, n)

            def turn(it, heads):
                for what, k, n in timeline(it, heads):
                    i, r = divmod(n, T)
                    s = k % U
                    if what == "b":
                        if n == 0:
                            pe.wait_ge(shifted[s], shifts(it, k))
                        j = key_order(i)[r]
                        g = k * UNITS + n
                        pe.wait_ge(exp_done, count(it, UNITS, g + (2 if (g - BSLOTS) % GROUP == 0 else 1)))
                        bank = SB[g % BSLOTS]
                        for v, c0, cn in block_pieces(j // BT, i, j):
                            used = KR if v == V - 1 else P
                            mm = pe.matmul(bank[:, c0:c0 + cn], rows(s, used, 1, v, P * j, P),
                                           rows(s, used, 0, v, QB * i + c0, cn),
                                           start=True, stop=True, skip_group_check=True)
                        mm.then_inc(b_raw if j // BT == i else b_plain, 1)
                    elif what == "shift":
                        j = key_order(i)[r]
                        if j // BT != i:
                            continue
                        pe.wait_ge(b_masked, count(it, T, k * T + diagonals(n) + 1))
                        c0 = P * (j % BT)
                        pe.matmul(SB[(k * UNITS + n) % BSLOTS][:, c0:c0 + P], stage[s][KR:SH, 1, 0, 0, 0:P],
                                  stage[s][KR:SH, 0, i, 0, c0:c0 + P], start=False, stop=True,
                                  skip_group_check=True).then_inc(b_diag, 1)
                    elif what == "a":
                        m = n + AHEAD
                        if m == UNITS:
                            pe.wait_ge(staged[(k + 2) % U], gathered(it, k + 2))
                        a_unit(it, k + 1 + m // UNITS, m % UNITS)
                    elif what == "maxima":
                        pe.wait_ge(ou_step, count(it, NB, NB * k + MAXIMA_SUMS + 1))
                        maxima(it, k + 1)
                    elif what == "base":
                        pe.wait_ge(ou_step, count(it, NB, NB * k + 1))
                        pe.wait_ge(nmT_ready, count(it, 1, k + 1))
                        base_product(it, k + U)
                    elif what == "pv":
                        i, r = divmod(GROUP * n, T)
                        if n == 0:
                            pe.wait_ge(mask_ready, count(it, 2, 2 * (k + 1)))
                        if r == 0:
                            pe.wait_ge(pv_out, count(it, NB, k * NB + i + 1))
                        pe.wait_ge(exp_done, count(it, UNITS, k * UNITS + GROUP * (n + 1) + BSLOTS))
                        for c in range(GROUP):
                            pe.matmul(PV[32 * c:32 * (c + 1), :], vh[:, s, key_order(i)[r + c], :],
                                      probs[:, (k * UNITS + GROUP * n + c) % PSLOTS, :],
                                      start=(r == 0), stop=(r == T - GROUP), skip_group_check=True)\
                                .then_inc(pv_used, 1)
                    elif what == "sum":
                        i, t = divmod(n, BT)
                        if t == 0:
                            pe.wait_ge(pv_out, count(it, NB, k * NB + i + 2))
                            pe.wait_ge(ou_step, count(it, NB, NB * k + i + 1))
                            if i == 0 and builds(it, k):
                                pe.wait_ge(base_ready, count(it, 1, k + U + 1))
                            if i == MAXIMA_SUMS and (it is not None or k + 1 < H):
                                pe.wait_ge(nmT_ready, count(it, 1, k + 2))
                        mm = pe.matmul(MISC[:, (D + 1) * t:(D + 1) * (t + 1)], pvs[:, i % 2, P * t:P * (t + 1)],
                                       groups[:], start=True, stop=True, skip_group_check=True)
                        if t == BT - 1:
                            mm.then_inc(pvs_free, 1)
            turns(pe, turn)

            pe.wait_ge(o_ready, H + 1)
            for g in range(NB):
                if g >= 2:
                    pe.wait_ge(oT_ready, g - 1)
                for t in range(BT):
                    mm = pe.transpose(SA[g % 2][:, P * t:P * (t + 1)], xn[:, BT * g + t, :], ident[:])
                mm.then_inc(oT_made, 1)
            for g in range(NB):
                pe.wait_ge(oT_ready, g + 1)
                if g >= 2:
                    pe.wait_ge(x1_ready, g - 1)
                for t in range(BT):
                    c = BT * g + t
                    mm = pe.matmul(SB[g % 2][:, P * t:P * (t + 1)], xT[:, P * c:P * (c + 1)], wo[:],
                                   start=True, stop=True, skip_group_check=True)
                mm.then_inc(wo_made, 1)
            def router_product(g):
                pe.wait_ge(x2T_ready, g + 1)
                pe.wait_ge(small_in, 16 * 5)
                for t in range(BT * g, BT * (g + 1)):
                    pe.matmul(SA[2][:, X * t:X * (t + 1)], x2T[:, P * t:P * (t + 1)], wrv,
                              start=True, stop=True, skip_group_check=True).then_inc(rt_made, 1)

            def split_product(bank, w_parts, x_parts, start, stop):
                for n, (w, x) in enumerate(((0, 0), (0, 1), (1, 0))):
                    mm = pe.matmul(bank[:, :], w_parts[w], x_parts[x],
                                   start=start and n == 0, stop=stop and n == 2, skip_group_check=True)
                return mm

            def up_product(g):
                i, u = divmod(g, X * FC)
                e, c = divmod(u, FC)
                if g == 0:
                    pe.wait_ge(w_split, 1)
                if g >= 3:
                    pe.wait_ge(up_out, g - 2)
                chunk, block = slice(P * c, P * (c + 1)), slice(QB * i, QB * (i + 1))
                split_product(SA[g % 3], (w1h[:, e, chunk], w1l[:, e, chunk]), (xH[:, block], xL[:, block]),
                              True, True).then_inc(up_made, 1)

            for g in range(NB):
                pe.wait_ge(normed, T + BT * (g + 1))
                if g >= 2:
                    pe.wait_ge(x2T_ready, g - 1)
                for t in range(BT):
                    mm = pe.transpose(SA[g % 2][:, P * t:P * (t + 1)], xn[:, BT * g + t, :], ident[:])
                mm.then_inc(transposed, 1)
                if g >= 1:
                    router_product(g - 1)
            router_product(NB - 1)
            pe.wait_ge(xL_ready, NB)
            up_product(0)
            up_product(1)
            pe.wait_ge(rt_step, RT_STEPS)
            for g in range(NB):
                if g >= 2:
                    pe.wait_ge(gT_ready, g - 1)
                for t in range(BT):
                    mm = pe.transpose(SB[g % 2][0:X, P * t:P * (t + 1)], gate[:, BT * g + t, :], ident[:])
                mm.then_inc(gT_made, 1)
            total = NB * X * FC

            def down_product(g):
                i, u = divmod(g, X * FC)
                e, c = divmod(u, FC)
                bank = (PV, MISC)[i % 2]
                if g == 0:
                    pe.wait_ge(w_split, 2)
                if u == 0:
                    if i >= 2:
                        pe.wait_ge(y_out, i - 1)
                    pe.wait_ge(gT_ready, NB)
                    pe.matmul(bank[:, :], b2v, gateT[0:X, QB * i:QB * (i + 1)], start=True, stop=False,
                              skip_group_check=True)
                pe.wait_ge(h_ready, g + 1)
                split_product(bank, (w2h[:, e, c, :], w2l[:, e, c, :]), (hH[g % 4], hL[g % 4]),
                              False, u == X * FC - 1).then_inc(h_free, 1)

            def y_transposes(i):
                pe.wait_ge(y_out, i + 1)
                if i >= 2:
                    pe.wait_ge(y_done, i - 1)
                for t in range(BT):
                    mm = pe.transpose(SB[i % 2][:, P * t:P * (t + 1)], yT[:, i, P * t:P * (t + 1)], ident[:])
                mm.then_inc(yT_made, 1)

            for g in range(total + DOWN_LAG):
                if 2 <= g < total:
                    up_product(g)
                if g >= DOWN_LAG:
                    down_product(g - DOWN_LAG)
                    if (g - DOWN_LAG) % (X * FC) == 5 and g > X * FC:
                        y_transposes((g - DOWN_LAG) // (X * FC) - 1)
            y_transposes(NB - 1)

        @block.vector
        def _(dve):
            dve.sem_inc(a_free, ASLOTS)
            dve.sem_inc(ou_step, 1)

            def step_of(s, count, ins):
                count[0] += 1
                ins.then_inc(s, 1)
                dve.wait_ge(s, count[0])

            for g in range(NB):
                dve.wait_ge(in_x[g], 16)
                for t in range(BT * g, BT * (g + 1)):
                    dve.bn_stats(stats[:, t, :], x[:, t, :]).then_inc(bn_done, 1)

            dve.wait_ge(in_t, 16 * 4)
            sm = [0]
            step_of(small, sm, dve.tensor_scalar(dec[:], dec[:], 0.01, 0.9999, ALU.max, ALU.min))
            step_of(small, sm, dve.tensor_tensor(mixs[:, 0, :], mixw[:, :, 0], mixw[:, :, 1], ALU.max))
            for n in range(N):
                step_of(small, sm, dve.tensor_tensor(mixw[:, :, n], mixw[:, :, n], mixs[:, 0, :], ALU.subtract))
            dve.wait_ge(small_act, 2)
            step_of(small, sm, dve.tensor_tensor(mixs[:, 0, :], mixw[:, :, 0], mixw[:, :, 1], ALU.add))
            step_of(small, sm, dve.reciprocal(mixs[:, 1, :], mixs[:, 0, :]))
            for n in range(N):
                step_of(small, sm, dve.tensor_tensor(mixt[:, :, 1 + n], mixw[:, :, n], mixs[:, 1, :], ALU.mult))
            step_of(small, sm, dve.tensor_scalar(mixs[:, 2, :], mixt[:, :, 1], cols[:, 5:6], cols[:, 1:2],
                                                 ALU.mult, ALU.add))
            step_of(small, sm, dve.scalar_tensor_tensor(mixt[:, :, 0], mixt[:, :, 2], cols[:, 6:7], mixs[:, 2, :],
                                                        ALU.mult, ALU.add))
            step_of(small, sm, dve.tensor_scalar(bqk[:], bqk[:], cols[:, 0:1], None, ALU.mult))
            dve.sem_inc(tables, 1)

            def statistics(src, g):
                for t in range(BT * g, BT * (g + 1)):
                    dve.bn_stats(stats[:, t, :], src[:, t, :]).then_inc(bn_done, 1)

            def normalise(src, part):
                dve.wait_ge(bn_done, 2 * T * part + T)
                for t in range(T):
                    dve.bn_aggr(mv[:, t, :], stats[:, t, :]).then_inc(bn_done, 1)
                dve.wait_ge(sqrt_done, part + 1)
                dve.reciprocal(rstd[:], rstd[:]).then_inc(rstd_ready, 1)
                dve.wait_ge(rstd_ready, part + 1)
                for t in range(T):
                    dve.tensor_scalar(xn[:, t, :], src[:, t, :], mv[:, t, 0:1], rstd[:, t:t + 1],
                                      ALU.subtract, ALU.mult).then_inc(normed, 1)

            normalise(x, 0)
            dve.wait_ge(in_c, n_consts)
            dve.tensor_copy(identb[:], ident[:])
            for g in range(NB):
                dve.wait_ge(v_made, g + 1)
                bank = (SA[0], SA[1], SA[2], SB[0])[g]
                for t in range(BT):
                    ins = dve.tensor_tensor(vals[:, BT * g + t, :, :].rearrange("p h d -> p (h d)"),
                                            bank[:, P * t:P * (t + 1)], bvo[:, 0, :], ALU.add)
                ins.then_inc(v_ready, 1)
            dve.wait_ge(v_ready, NB)
            dve.wait_ge(ones_set, 2)
            build_vectors(dve, None, 0)

            def a_max(it, k, n):
                i, b = divmod(n, NB)
                g = k * UNITS + n
                bank = SA[g % ASLOTS]
                dve.wait_ge(a_made, count(it, UNITS, g + 1))
                if b == i // BT:
                    if n == 0:
                        dve.wait_ge(mask_ready, count(it, 2, 2 * (k + 1)))
                    tile = bank[:, P * (i % BT):P * (i % BT + 1)]
                    dve.tensor_tensor(tile, tile, masks[:, k % U, :], ALU.mult).then_inc(a_masked, 1)
                    dve.wait_ge(a_masked, count(it, T, k * T + i + 1))
                dve.tensor_reduce(mx[:, n:n + 1], bank[:, :], AX.X, ALU.max).then_inc(a_free, 1)

            def finish(it, k):
                c = [0]

                def link(ins):
                    c[0] += 1
                    ins.then_inc(nm_step, 1)
                    dve.wait_ge(nm_step, count(it, 5, 5 * k + c[0]))
                dve.wait_ge(a_free, count(it, UNITS, (k + 1) * UNITS + ASLOTS))
                link(dve.tensor_reduce(nm[:, 0, :], mx[:].rearrange("p (t b) -> p t b", b=NB), AX.X, ALU.max,
                                       negate=True))
                whole, rest = (nm[:, x, :].rearrange("p (b t) -> p b t", t=BT) for x in range(2))
                link(dve.tensor_copy(nmp[:, :, 0, :], whole))
                link(dve.tensor_tensor(rest, whole, nmp[:, :, 0, :], ALU.subtract))
                link(dve.tensor_copy(nmp[:, :, 1, :], rest))
                link(dve.tensor_tensor(nmp[:, :, 2, :], rest, nmp[:, :, 1, :], ALU.subtract))

            def maxima_out(it, k):
                dve.wait_ge(nmT_made, count(it, 1, k + 1))
                if it is not None or k >= 1:
                    dve.wait_ge(shifted[(k - 1) % U], shifts(it, k - 1))
                dve.tensor_copy(nmT[:], MISC[:, :].bitcast(BF16)[0:3 * T, 0:P]).then_inc(nmT_ready, 1)

            def first_maxima():
                for n in range(UNITS):
                    a_max(None, 0, n)
                finish(None, 0)
                maxima_out(None, 0)
                for n in range(AHEAD):
                    a_max(None, 1, n)

            first_maxima()

            def mask(it, k, n):
                i, r = divmod(n, T)
                j = key_order(i)[r]
                if j // BT != i:
                    return
                c0 = P * (j % BT)
                tile = SB[(k * UNITS + n) % BSLOTS][:, c0:c0 + P]
                dve.wait_ge(b_raw, count(it, T, k * T + diagonals(n) + 1))
                dve.tensor_tensor(tile, tile, masks[:, k % U, :], ALU.mult).then_inc(b_masked, 1)

            def turn(it, heads):
                units = [(k, n) for k in heads for n in range(UNITS)]
                order = timeline(it, heads)
                for u in range(EARLY):
                    mask(it, *units[u])
                for what, k, n in order:
                    if what == "b":
                        u = (k - heads[0]) * UNITS + n + EARLY
                        if u < len(units):
                            mask(it, *units[u])
                    elif what == "a":
                        m = n + AHEAD
                        a_max(it, k + 1 + m // UNITS, m % UNITS)
                        if m == UNITS - 1:
                            finish(it, k + 1)
                    elif what == "maxima":
                        maxima_out(it, k + 1)
                    elif what == "sum" and n % BT == BT - 1:
                        i = n // BT
                        dve.wait_ge(pvs_free, count(it, NB, k * NB + i + 3))
                        if i == 0:
                            dve.wait_ge(o_ready, count(it, 1, k + 1))
                        dve.tensor_copy(ou[:, BT * i:BT * (i + 1), :],
                                        MISC[:, 0:BT * (D + 1)].rearrange("p (t d) -> p t d", t=BT))\
                            .then_inc(ou_step, 1)
                        if i == NB - 1:
                            dve.wait_ge(ou_step, count(it, NB, NB * (k + 1) + 1))
                            dve.reciprocal(rz[:], ou[:, :, D]).then_inc(rz_ready, 1)
            turns(dve, turn)

            dve.wait_ge(x1_biased, 1)
            for g in range(NB):
                dve.wait_ge(wo_made, g + 1)
                rows = x1[:, BT * g:BT * (g + 1), :]
                dve.tensor_tensor(rows, rows, SB[g % 2][:, :].rearrange("p (t e) -> p t e", e=E), ALU.add)\
                   .then_inc(x1_ready, 1)
                dve.wait_ge(x1_ready, g + 1)
                statistics(x1, g)
            normalise(x1, 1)
            for g in range(NB):
                block = slice(QB * g, QB * (g + 1))
                dve.wait_ge(xT_ready, NB + g + 1)
                dve.tensor_tensor(xL[:, block], x2T[:, block], xH[:, block].bitcast(F32), ALU.subtract)\
                    .then_inc(xL_ready, 1)

            c = [0]

            def link(ins):
                step_of(rt_step, c, ins)

            dve.wait_ge(rt_made, T)
            dve.wait_ge(small_in, 16 * 5)
            dve.tensor_tensor(lg[:], SA[2][:, 0:T * X].rearrange("p (t x) -> p t x", x=X),
                              brv.unsqueeze(1).broadcast_to([P, T, X]), ALU.add).then_inc(lg_ready, 1)
            dve.wait_ge(lg_ready, 1)
            link(dve.tensor_reduce(rt1, lg[:], AX.X, ALU.max))
            link(dve.tensor_tensor(lg[:], lg[:], widen(rt1, X), ALU.subtract))
            dve.wait_ge(rt_act, 1)
            link(dve.tensor_reduce(rt1, lg[:], AX.X, ALU.add))
            link(dve.reciprocal(rt2, rt1))
            link(dve.tensor_tensor(lg[:], lg[:], widen(rt2, X), ALU.mult))
            mine = lg.unsqueeze(3).broadcast_to([P, T, X, X])
            theirs = lg.unsqueeze(2).broadcast_to([P, T, X, X])
            tie = tiev.unsqueeze(1).broadcast_to([P, T, X, X])
            link(dve.tensor_tensor(big1, theirs, mine, ALU.is_equal))
            link(dve.tensor_tensor(big1, big1, tie, ALU.mult))
            link(dve.tensor_tensor(big2, theirs, mine, ALU.is_gt))
            link(dve.tensor_tensor(big1, big1, big2, ALU.add))
            link(dve.tensor_tensor(big1, big1, theirs, ALU.mult))
            link(dve.tensor_reduce(cum, big1, AX.X, ALU.add))
            link(dve.tensor_scalar(eq0, cum, 0.0, None, ALU.is_equal))
            link(dve.tensor_tensor(cum, cum, lg[:], ALU.add))
            link(dve.tensor_scalar(cum, cum, TOP_P, None, ALU.is_lt))
            link(dve.tensor_tensor(cum, cum, eq0, ALU.max))
            link(dve.tensor_tensor(gate, cum, lg[:], ALU.mult))

            def add_y(i):
                dve.wait_ge(yT_made, i + 1)
                rows = x1[:, BT * i:BT * (i + 1), :]
                dve.tensor_tensor(rows, rows, SB[i % 2][:, :].rearrange("p (t e) -> p t e", e=E), ALU.add)\
                   .then_inc(y_done, 1)

            for i in range(NB):
                for u in range(X * FC):
                    if u == 0:
                        dve.wait_ge(g_in[2 * i], 16)
                    if u == FIRST_GATES * FC:
                        dve.wait_ge(g_in[2 * i + 1], 16)
                    g = i * X * FC + u
                    dve.wait_ge(up_out, g + 1)
                    dve.tensor_tensor(up[g % 4], up[g % 4], gates[i][:, u // FC, :], ALU.mult)\
                        .then_inc(up_scaled, 1)
                    if i >= 1 and u == DOWN_LAG + 8:
                        add_y(i - 1)
            add_y(NB - 1)



DOWN_LAG = 4
FIRST_GATES = 2
RT_STEPS = 16


def kernel(**inputs):
    import concourse.bacc as _bacc
    from concourse.bass_utils import run_bass_kernel_spmd as _run

    g = {k.split("_", 1)[1]: np.asarray(v) for k, v in inputs.items()}

    def everywhere(v):
        return np.broadcast_to(v, (P,) + v.shape)

    def qk_rows(q, k):
        q, k = (np.repeat(m.reshape(H, 1, D, -1), N, 1) for m in (q, k))
        return np.stack([q, k], 1).reshape(H, 2 * ROWS, -1)

    wqk = qk_rows(g["attn_Wq"], g["attn_Wk"]).transpose(2, 0, 1)
    bqk = np.tile(qk_rows(g["attn_bq"], g["attn_bk"])[:, :, 0].T, (NB, 1))
    dec = g["attn_decay_params"]
    by_row = np.tile(np.repeat(dec.T, D, 0), (2 * NB, 1))
    token = np.arange(S).reshape(NB, 1, QB)
    dist = np.stack([np.abs(token % (2 * w) - w) for w in WIDTHS], 1).reshape(NB, 1, LV * QB)
    lane = np.arange(P)
    query, second = lane // ROWS % 2 == 0, lane // D % 2 == 1
    cols = np.zeros((P, 8), np.float32)
    cols[:, 0] = np.where(query, D ** -0.5, 1)
    cols[:, 1] = ~query
    cols[:, 2] = np.where(query, 1 / N, 1)
    cols[:, 4] = EPS
    cols[:, 5] = query & ~second
    cols[:, 6] = query & second
    lower = np.arange(X)[None, :] < np.arange(X)[:, None]
    arrays = {
        "x": g["attn_x"].reshape(S, E),
        "wqk": wqk, "bqk": bqk, "wv": g["attn_Wv"].T, "wo": g["attn_Wo"].T,
        "bvo": everywhere(np.stack([g["attn_bv"], g["attn_bo"]])),
        "dec": np.concatenate([by_row, everywhere(dec.reshape(-1))], 1),
        "mix": everywhere(g["attn_mix_weights"]),
        "wr": g["ffn_Wr"], "br": everywhere(g["ffn_br"]),
        "w1": g["ffn_W1"].transpose(1, 0, 2),
        "b1": g["ffn_b1"].reshape(X, FC, P).transpose(2, 0, 1),
        "w2": g["ffn_W2"].reshape(X, FC, P, E).transpose(2, 0, 1, 3),
        "b2": g["ffn_b2"],
        "c_ident": np.eye(P, dtype=np.float32),
        "c_cols": cols,
        "c_groups": np.tile(np.eye(2 * ROWS, D + 1, dtype=np.float32), (NB, 1)),
        "c_dist": np.broadcast_to(dist, (NB, 2 * ROWS, LV * QB)).reshape(P, LV * QB).astype(np.float16),
        "c_absd": np.abs(lane[:, None] - lane[None, :]).astype(np.float32),
        "c_rest": np.repeat([1.0, 0.0], (SH - KR, P - SH)).reshape(-1, 1, 1, 1).repeat(NB, 1)
        .repeat(V, 2).repeat(QB, 3).astype(mybir.dt.np(BF16)),
        "c_tie": everywhere(lower.astype(np.float32)),
    }
    nc = _bacc.Bacc("TRN2", target_bir_lowering=False, num_devices=1)
    aps, feed = {}, {}
    for name, v in arrays.items():
        feed[f"in_{name}"] = np.ascontiguousarray(v)
        aps[name] = nc.dram_tensor(f"in_{name}", v.shape, mybir.dt.from_np(v.dtype), kind="ExternalInput").ap()
    aps["scratch"] = nc.dram_tensor("scratch", (X, S), F32, kind="Internal").ap()
    out = nc.dram_tensor("out", (S, E), F32, kind="ExternalOutput").ap()
    build_program(nc, aps, out)
    r = _run(nc, [feed], core_ids=[0])
    return r.results[0]["out"].reshape(1, S, E)
```
